# Optimizing a Trainium2 kernel written in Bass

```python
import numpy as np
import jax
import jax.numpy as jnp

def _softmax(x, axis=-1):
    return jax.nn.softmax(x, axis=axis)
def _gelu(x):
    return jax.nn.gelu(x, approximate=True)
def _silu(x):
    return jax.nn.silu(x)
def _sigmoid(x):
    return jax.nn.sigmoid(x)
def _layernorm(x, axis=-1, eps=1e-5):
    m = jnp.mean(x, axis=axis, keepdims=True)
    v = jnp.var(x, axis=axis, keepdims=True)
    return (x - m) / jnp.sqrt(v + eps)
def _scatter_add(tgt, idx, src, axis=0):
    return tgt.at[idx].add(src)
def _segment_sum(src, seg, n):
    return jax.ops.segment_sum(src, seg, n)

kernel_name = 'mk_conv_attn_hybrid_d2_conv_nchw128_ebcd05'

def setup_inputs(seed: int = 0):
    np.random.seed(seed)
    _w = jnp.asarray
    def _rec_inputs():
        import jax
        import jax.numpy as jnp
        _gk = jax.random.key(seed)
        x = -0.0005207 + 1.001 * jax.random.normal(jax.random.fold_in(_gk, 1), (4, 128, 64, 64), jnp.float32)
        return x
    x = _rec_inputs()
    def _L0_conv_setup():
        import jax, jax.numpy as jnp
        import numpy as np

        def _prelu(x, a):
            return jnp.where(x >= 0, x, a * x)

        def _conv1x1(x, w, b, a):
            y = jnp.einsum('oc,nchw->nohw', w, x) + b[None, :, None, None]
            return _prelu(y, a)
        key = jax.random.key(seed)
        ks = jax.random.split(key, 8)
        N, C, H, W = (4, 128, 64, 64)
        Cr = C // 2
        sC = 1.0 / np.sqrt(C)
        x = jax.random.normal(ks[0], (N, C, H, W), dtype=jnp.float32)
        w1 = jax.random.normal(ks[1], (Cr, C), dtype=jnp.float32) * sC
        b1 = jnp.zeros((Cr,), dtype=jnp.float32)
        a1 = jnp.asarray(0.25, dtype=jnp.float32)
        w2 = jax.random.normal(ks[2], (Cr, C), dtype=jnp.float32) * sC
        b2 = jnp.zeros((Cr,), dtype=jnp.float32)
        a2 = jnp.asarray(0.25, dtype=jnp.float32)
        wa = jax.random.normal(ks[3], (C, C), dtype=jnp.float32) * sC
        ba = jnp.zeros((C,), dtype=jnp.float32)
        aa = jnp.asarray(0.25, dtype=jnp.float32)
        return {'x': x, 'w1': w1, 'b1': b1, 'a1': a1, 'w2': w2, 'b2': b2, 'a2': a2, 'wa': wa, 'ba': ba, 'aa': aa}
    _L0_conv_all = _L0_conv_setup()
    _L0_conv_in = {k: v for k, v in _L0_conv_all.items() if k in ('w1', 'b1', 'a1', 'w2', 'b2', 'a2', 'wa', 'ba', 'aa', )}
    del _L0_conv_all

    def _L1_attn_setup():
        import jax, jax.numpy as jnp
        import numpy as np
        B, S, H, A = (8, 1024, 128, 16)
        key = jax.random.key(seed)
        ks = jax.random.split(key, 5)
        scale = 1.0 / np.sqrt(2 * H)
        return {'x': jax.random.normal(ks[0], (B, S, H), dtype=jnp.float32), 'W1': jax.random.normal(ks[1], (2 * H, A), dtype=jnp.float32) * scale, 'b1': jax.random.normal(ks[2], (A,), dtype=jnp.float32) * scale, 'w2': jax.random.normal(ks[3], (A, 1), dtype=jnp.float32) * (1.0 / np.sqrt(A)), 'b2': jax.random.normal(ks[4], (1,), dtype=jnp.float32) * (1.0 / np.sqrt(A))}
    _L1_attn_all = _L1_attn_setup()
    _L1_attn_in = {k: v for k, v in _L1_attn_all.items() if k in ('W1', 'b1', 'w2', 'b2', )}
    del _L1_attn_all

    def _L1_ffn_setup():
        import jax, jax.numpy as jnp
        import numpy as np
        B, S, D, E, H, O, K = (512, 2048, 128, 64, 512, 128, 8)
        key = jax.random.key(seed)
        k0, k1, k2, k3 = jax.random.split(key, 4)
        x = jax.random.normal(k0, (B, S, D), dtype=jnp.float32)
        gate_w = jax.random.normal(k1, (E, D), dtype=jnp.float32) * (1.0 / np.sqrt(D))
        gate_b = jnp.zeros((E,), dtype=jnp.float32)
        weight1 = jax.random.uniform(k2, (E, D + 1, H), dtype=jnp.float32, minval=-1.0, maxval=1.0) * (1.0 / np.sqrt(D + 1))
        weight2 = jax.random.uniform(k3, (E, H + 1, O), dtype=jnp.float32, minval=-1.0, maxval=1.0) * (1.0 / np.sqrt(H + 1))
        return {'x': x, 'gate_w': gate_w, 'gate_b': gate_b, 'weight1': weight1, 'weight2': weight2}
    _L1_ffn_all = _L1_ffn_setup()
    _L1_ffn_in = {k: v for k, v in _L1_ffn_all.items() if k in ('gate_w', 'gate_b', 'weight1', 'weight2', )}
    del _L1_ffn_all

    return {
        "x": x,
        "L0_conv_w1": _L0_conv_in["w1"],
        "L0_conv_b1": _L0_conv_in["b1"],
        "L0_conv_a1": _L0_conv_in["a1"],
        "L0_conv_w2": _L0_conv_in["w2"],
        "L0_conv_b2": _L0_conv_in["b2"],
        "L0_conv_a2": _L0_conv_in["a2"],
        "L0_conv_wa": _L0_conv_in["wa"],
        "L0_conv_ba": _L0_conv_in["ba"],
        "L0_conv_aa": _L0_conv_in["aa"],
        "L1_attn_W1": _L1_attn_in["W1"],
        "L1_attn_b1": _L1_attn_in["b1"],
        "L1_attn_w2": _L1_attn_in["w2"],
        "L1_attn_b2": _L1_attn_in["b2"],
        "L1_ffn_gate_w": _L1_ffn_in["gate_w"],
        "L1_ffn_gate_b": _L1_ffn_in["gate_b"],
        "L1_ffn_weight1": _L1_ffn_in["weight1"],
        "L1_ffn_weight2": _L1_ffn_in["weight2"],
    }

def reference(x, L0_conv_w1, L0_conv_b1, L0_conv_a1, L0_conv_w2, L0_conv_b2, L0_conv_a2, L0_conv_wa, L0_conv_ba, L0_conv_aa, L1_attn_W1, L1_attn_b1, L1_attn_w2, L1_attn_b2, L1_ffn_gate_w, L1_ffn_gate_b, L1_ffn_weight1, L1_ffn_weight2):
    import jax
    import jax.numpy as jnp
    def _L0_conv_ref(x, w1, b1, a1, w2, b2, a2, wa, ba, aa):
        import jax, jax.numpy as jnp
        import numpy as np

        def _prelu(x, a):
            return jnp.where(x >= 0, x, a * x)

        def _conv1x1(x, w, b, a):
            y = jnp.einsum('oc,nchw->nohw', w, x) + b[None, :, None, None]
            return _prelu(y, a)
        N, C, H, W = x.shape
        HW = H * W
        e1 = _conv1x1(x, w1, b1, a1).reshape(N, -1, HW)
        e2 = _conv1x1(x, w2, b2, a2).reshape(N, -1, HW)
        asm = _conv1x1(x, wa, ba, aa).reshape(N, C, HW)
        score = jnp.einsum('nci,ncj->nij', e1, e2)
        score = jax.nn.softmax(score, axis=2)
        out = jnp.einsum('nij,ncj->nci', score, asm)
        return out.reshape(N, C, H, W)

    def _L1_attn_ref(x, W1, b1, w2, b2):
        import jax, jax.numpy as jnp
        import numpy as np
        B, S, H, A = (8, 1024, 128, 16)
        h = x.shape[-1]
        f = jnp.einsum('bih,ha->bia', x, W1[:h])
        g = jnp.einsum('bjh,ha->bja', x, W1[h:])
        t = jnp.tanh(f[:, :, None, :] + g[:, None, :, :] + b1)
        scores = jnp.einsum('bija,a->bij', t, w2[:, 0]) + b2[0]
        n_seq = x.shape[1]
        flag = jnp.tril(jnp.ones((n_seq, n_seq), dtype=x.dtype), -1)[None, :, :]
        e = jnp.exp(scores) * flag
        denom = jnp.sum(e, axis=-1, keepdims=True) + 1e-10
        w = e / denom
        return jnp.einsum('bij,bjh->bih', w, x)

    def _L1_ffn_ref(x, gate_w, gate_b, weight1, weight2):
        import jax, jax.numpy as jnp
        import numpy as np
        B, S, D, E, H, O, K = (512, 2048, 128, 64, 512, 128, 8)
        Bn, Sn, Dn = x.shape
        logits = jnp.einsum('bsd,ed->bse', x, gate_w) + gate_b
        probs = jax.nn.softmax(logits, axis=1)
        vals, idx = jax.lax.top_k(probs.transpose(0, 2, 1), K)
        topv = vals.transpose(0, 2, 1)
        topi = idx.transpose(0, 2, 1)
        flat_idx = topi.reshape(Bn, K * E)
        gathered = jnp.take_along_axis(x, flat_idx[:, :, None], axis=1)
        gathered = gathered.reshape(Bn, K, E, Dn)
        pooled = jnp.einsum('bked,bke->bed', gathered, topv)
        ones = jnp.ones((E, Bn, 1), dtype=x.dtype)
        h = jnp.concatenate([pooled.transpose(1, 0, 2), ones], axis=-1)
        h = jax.nn.gelu(jnp.einsum('ebd,edh->ebh', h, weight1), approximate=False)
        h = jnp.concatenate([h, ones], axis=-1)
        out = jnp.einsum('ebh,eho->ebo', h, weight2)
        out = out.transpose(1, 0, 2)
        weighted = jnp.einsum('beo,bke->bkeo', out, topv).reshape(Bn, K * E, O)
        outputs = jnp.zeros((Bn, Sn, O), dtype=x.dtype)
        outputs = outputs.at[jnp.arange(Bn)[:, None], flat_idx].add(weighted)
        return outputs

    def _gn(v, G=32, eps=1e-5):
        B_, C_, H_, W_ = v.shape
        g = v.reshape(B_, G, C_ // G, H_, W_)
        m = jnp.mean(g, axis=(2, 3, 4), keepdims=True)
        s = jnp.var(g, axis=(2, 3, 4), keepdims=True)
        return ((g - m) / jnp.sqrt(s + eps)).reshape(v.shape)

    def _ln_c(v, eps=1e-6):
        m = jnp.mean(v, axis=1, keepdims=True)
        s = jnp.var(v, axis=1, keepdims=True)
        return (v - m) / jnp.sqrt(s + eps)

    def _ln_t(v, eps=1e-5):
        m = jnp.mean(v, axis=-1, keepdims=True)
        s = jnp.var(v, axis=-1, keepdims=True)
        return (v - m) / jnp.sqrt(s + eps)

    def _to_tokens(v):
        B_, C_, H_, W_ = v.shape
        return v.reshape(B_, C_, H_ * W_).transpose(0, 2, 1)
    def _from_tokens(t, like):
        B_, C_, H_, W_ = like.shape
        return t.transpose(0, 2, 1).reshape(B_, C_, H_, W_)

    x = x + _L0_conv_ref(_gn(x), L0_conv_w1, L0_conv_b1, L0_conv_a1, L0_conv_w2, L0_conv_b2, L0_conv_a2, L0_conv_wa, L0_conv_ba, L0_conv_aa)
    t = _to_tokens(x)
    t = t + _L1_attn_ref(_ln_t(t), L1_attn_W1, L1_attn_b1, L1_attn_w2, L1_attn_b2)
    t = t + _L1_ffn_ref(_ln_t(t), L1_ffn_gate_w, L1_ffn_gate_b, L1_ffn_weight1, L1_ffn_weight2)
    x = _from_tokens(t, x)
    return x


_drawn_inputs = setup_inputs


def setup_inputs(seed=0):
    import zlib

    import numpy as np

    out = dict(_drawn_inputs(seed))
    spreads = {'L0_conv_b1': (0.0, 0.1),
     'L0_conv_b2': (0.0, 0.1),
     'L0_conv_ba': (0.0, 0.1),
     'L1_ffn_gate_b': (0.0, 0.1)}
    factors = {'L1_attn_b1': 8.0, 'L1_ffn_gate_w': 8.0, 'L1_ffn_weight1': 8.0, 'L1_ffn_weight2': 8.0}
    for name, (base, spread) in spreads.items():
        noise = np.random.default_rng([zlib.crc32(name.encode()), seed]).standard_normal(out[name].shape)
        drawn = base * np.exp(spread * noise) if base else spread * noise
        out[name] = jnp.asarray(drawn.astype(out[name].dtype))
    for name, factor in factors.items():
        out[name] = (out[name] * factor).astype(out[name].dtype)
    return out
```

```python
import concourse.bass as bass
from concourse import mybir
from contextlib import ExitStack

BATCH, CH, TOK = 4, 128, 4096
HALF = CH // 2
CHUNK = 512
NCH = TOK // CHUNK
BLK = 128
NBLK = TOK // BLK
PER = CHUNK // BLK
AH = 16
KEYS = CH // AH
UNITS = 4
EXP, HID, OUT = 64, 512, 128
GRP = EXP // 4
GN_EPS, LN_EPS, DEN_EPS = 1e-5, 1e-5, 1e-10

_COLS = [("ident", 128), ("gmat", 128), ("tri", 128), ("w12", 128), ("wa", 128), ("gw", 64), ("w1a", 128),
         ("w1b", 8 * 128), ("w2k", 4 * 32), ("ba", 128), ("b12", 1), ("a12", 1), ("b1", 1), ("b2", 1),
         ("aa", 1), ("gb", 1)]
_AT, _n = {}, 0
for _k, _w in _COLS:
    _AT[_k] = (_n, _n + _w)
    _n += _w
NPACK = _n


def blocks_before(c):
    return PER * c * (c + 1) // 2


NB = blocks_before(NCH)


class Block:

    def __init__(self, n, c, jb, diag, first, last):
        self.n, self.c, self.jb, self.diag, self.first, self.last = n, c, jb, diag, first, last
        self.off = 0 if diag is None else BLK * diag
        self.par = self.ring = None


def each_block(eng, emit):
    prev = None
    for c in range(NCH):
        n0, full = blocks_before(c), PER * c

        def blk(jb, ring, diag=None):
            x = Block(n0 + jb, c, jb, diag, isinstance(jb, int) and jb == 0, diag == PER - 1)
            x.par, x.ring = ring % 2, ring
            return x

        if full:
            for u in range(PER):
                cur = blk(u, u)
                emit(cur, prev)
                prev = cur
        if c > 1:
            with eng.Fori(1, c) as h:
                for u in range(PER):
                    cur = blk(PER * h + u, u)
                    emit(cur, blk(PER * h + u - 1, (u - 1) % PER))
            prev = blk(full - 1, PER - 1)
        for d in range(PER):
            cur = blk(full + d, d, d)
            emit(cur, prev)
            prev = cur
    emit(None, prev)


def hybrid_kernel(nc, x, pack, sel, w1, w2, b1all, b2all, out, y2_dram, p_dram, eo_dram):
    f32, bf16 = mybir.dt.float32, mybir.dt.bfloat16
    ALU = mybir.AluOpType
    ACT = mybir.ActivationFunctionType
    AXX = mybir.AxisListType.X
    ctx = ExitStack()
    with ctx:
        def sb(name, shape):
            return ctx.enter_context(nc.sbuf_tensor(name, shape, f32))

        def sem(name):
            return ctx.enter_context(nc.semaphore(name))

        PK = sb("packed", [128, NPACK])
        X = sb("x_channels", [128, TOK])
        XN = sb("normed_channels", [128, TOK])
        E1 = sb("e1_and_minus_max", [HALF + 1, TOK])
        E2 = sb("e2_and_ones", [HALF + 1, TOK])
        VT = sb("asm_tokens", [128, NBLK, 128])
        XT = sb("normed_tokens", [128, NBLK, 128])
        F = sb("query_part", [128, TOK])
        S = sb("tanh_slots", [128, UNITS, 4, CHUNK])
        EB = sb("exp_scores", [128, 2, CHUNK])
        DS = sb("exp_sums", [128, 2, CHUNK])
        ACCS = sb("context_copy", [128, CHUNK])
        RD = sb("recip_denominator", [128, CHUNK])
        B = sb("key_part", [128, TOK // KEYS])
        BR = sb("key_part_ring", [128, PER, CH // KEYS])
        XR = sb("value_ring", [128, PER, 128])
        ONES = sb("ones", [128, 128])
        MX = sb("row_max", [128, NBLK, 4])
        M1 = sb("row_max_all", [128, NBLK])
        NM = sb("minus_max_rows", [NBLK, 128])
        ST = sb("stats", [128, NBLK, 6])
        MV = sb("mean_var", [128, NBLK, 2])
        RS = sb("rstd", [128, NBLK])
        SM = sb("small", [128, 16])
        TOP = sb("top8", [EXP, 8])
        PL = sb("pooled", [128, EXP, BATCH])
        T1 = sb("tmp_low", [128, CHUNK])
        T2 = sb("tmp_high", [128, CHUNK])
        SELB = sb("expert_select", [EXP, EXP * 32])
        B1A = sb("ffn_bias1", [EXP, HID])
        B2A = sb("ffn_bias2", [EXP, OUT])
        W1G = sb("ffn_w1", [128, 2, 4, HID])
        flat = S[:, :, :, :].rearrange("p a b c -> p (a b c)")
        PROB = flat[:, 0:4096].rearrange("p (s u n) -> p s u n", s=2, u=4)
        PSUMS = flat[:, 4096:6144].rearrange("p (u n) -> p u n", u=4)
        PT = flat[:, 0:NBLK * EXP].rearrange("p (k e) -> p k e", e=EXP)
        LOG, REM, SELP = E1[0:EXP, :], E2[0:EXP, :], F[0:EXP, :]
        W2G = XN[:, :].rearrange("p (s e c o) -> p s e c o", s=2, e=4, c=4)
        HS = X[:, 0:HID]
        HT = X[:, 1024:1536].rearrange("p (c m) -> p c m", c=4)
        ES = VT[:, 0:GRP, :]
        EO = XT[0:EXP, 0:BATCH, :]
        YF = [F[:, :], flat[:, 0:TOK]]
        PF = [E1[0:EXP, :], E2[0:EXP, :]]
        half = F[:, :].bitcast(bf16)
        E1P, E2H = half[:, 0:TOK], half[:, TOK:2 * TOK]
        E2M = XT[:, :, :].rearrange("p a b -> p (a b)").bitcast(bf16)[:, 0:TOK]
        PS = ctx.enter_context(nc.psum_tensor("ps", [128, 8, 512], f32))
        ACC, DEN = PS[:, 4, :], PS[:, 5, :]

        def pk(k, rows=128):
            a, z = _AT[k]
            return PK[0:rows, a:z]

        w1b = pk("w1b").rearrange("p (r m) -> p r m", r=KEYS)
        w2k = pk("w2k").rearrange("p (k m) -> p k m", k=4)

        s_const = sem("consts_loaded")
        s_ones = sem("ones_set")
        s_x = sem("x_loaded")
        s_y2 = sem("y2_saved")
        s_p = sem("probs_saved")
        s_alone = sem("waits_alone")
        s_v = sem("vector_step")
        s_chst = sem("channel_stats_ready")
        s_chsq = sem("channel_squares_ready")
        s_var = sem("variance_ready")
        s_sd = sem("stddev_ready")
        s_xn = sem("gn_ready")
        s_wr = [sem(f"work_bank_ready{i}") for i in range(2)]
        s_wf = [sem(f"work_bank_free{i}") for i in range(2)]
        s_e12 = sem("projections_ready")
        s_ec = sem("e_chunk_ready")
        s_eh = sem("e_high_parts_ready")
        s_mxq = sem("max_scores_ready")
        s_mxd = sem("max_scores_used")
        s_m1 = sem("row_max_ready")
        s_nm = sem("minus_max_ready")
        s_nmr = sem("minus_max_row_loaded")
        s_qk = sem("conv_scores_ready")
        s_pe = sem("conv_probs_ready")
        s_pv = sem("conv_probs_used")
        s_ps = sem("conv_sums_added")
        s_cc = sem("conv_chunk_ready")
        s_ac = sem("conv_acc_copied")
        s_cd = sem("conv_den_used")
        s_cm = sem("conv_scaled")
        s_cx = sem("conv_residual_added")
        s_xt = sem("tokens_ready")
        s_xc = sem("channels_ready")
        s_fr = sem("query_part_ready")
        s_kr = sem("key_part_ready")
        s_br = sem("key_ring_ready")
        s_xr = sem("value_ring_ready")
        s_sum = sem("sums_ready")
        s_th = sem("tanh_ready")
        s_tu = sem("tanh_used")
        s_ex = sem("exp_ready")
        s_mk = sem("exp_masked")
        s_ep = sem("exp_used_by_product")
        s_es = sem("exp_used_by_sum")
        s_dc = sem("context_chunk_ready")
        s_da = sem("context_copied")
        s_dd = sem("denominator_used")
        s_dx = sem("context_added")
        s_l = sem("logits_ready")
        s_lx = sem("gate_max_ready")
        s_le = sem("gate_exp_ready")
        s_sp = sem("selected_ready")
        s_pt = sem("selected_tokens_ready")
        s_pl = sem("pooled_ready")
        s_w = [sem(f"ffn_weights_loaded{i}") for i in range(2)]
        s_wu = sem("ffn_weights_used")
        s_h = sem("ffn_hidden_ready")
        s_g = sem("ffn_gelu_ready")
        s_ht = sem("ffn_hidden_transposed")
        s_htc = sem("ffn_hidden_copied")
        s_o = sem("ffn_out_ready")
        s_oc = sem("ffn_out_copied")
        s_eo = sem("expert_out_saved")
        s_eol = sem("expert_out_loaded")
        s_fl = [sem(f"final_inputs_loaded{i}") for i in range(2)]
        s_fm = sem("final_product_ready")
        s_fa = sem("final_added")
        s_out = [sem(f"out_saved{i}") for i in range(2)]

        W_GN = 0
        W_E = 2
        W_M = W_E + 2 * NCH
        W_T = W_M + 2
        W_C = W_T + NCH
        W_F = W_C + NCH
        W_B = W_F + NCH
        W_T2 = W_B + 2
        W_C2 = W_T2 + NCH
        W_L = W_C2 + NCH
        W_P = W_L + NCH
        W_PL = W_P + 4
        NW = W_PL + 2
        SKIPPED = [W_M + 1, W_B + 1, W_PL + 1]

        def bank(k):
            return PS[:, 6 + k % 2, :]

        def uses_before(k):
            return sum(1 for i in range(k % 2, k, 2) if i not in SKIPPED)

        UPB = [uses_before(NW), uses_before(NW + 1)]

        def bank_ready(eng, b, k):
            eng.wait_ge(s_wr[k % 2], b * UPB[k % 2] + uses_before(k) + 1)

        def bank_free(eng, b, k):
            eng.wait_ge(s_wf[k % 2], b * UPB[k % 2] + uses_before(k) + 1)

        def wait_alone(eng, sm, value):
            eng.wait_ge(sm, value)
            eng.sem_inc(s_alone, 1)

        block = ctx.enter_context(nc.Block())

        @block.sync
        def _(sp):
            sp.dma_start(PK[:, :], pack).then_inc(s_const, 16)
            sp.dma_start(SELB[:, :], sel).then_inc(s_const, 16)
            sp.dma_start(B1A[:, :], b1all).then_inc(s_const, 16)
            sp.dma_start(B2A[:, :], b2all).then_inc(s_const, 16)
            with sp.Fori(0, BATCH) as b:
                sp.wait_ge(s_y2, b * 16 + 16)
                sp.wait_ge(s_p, b * 16 + 16)
                sp.dma_start(X[:, :], x[bass.ds(b, 1), :, :].rearrange("a c t -> (a c) t")).then_inc(s_x, 16)
                sp.wait_ge(s_nm, b + 1)
                sp.dma_start(E1[HALF:HALF + 1, :], NM[:, :]).then_inc(s_nmr, 16)
                sp.wait_ge(s_dx, (b + 1) * NCH)
                sp.dma_start(y2_dram[bass.ds(b, 1), :, :].rearrange("a c t -> (a c) t"), X[:, :]).then_inc(s_y2, 16)
                sp.wait_ge(s_sp, b + 1)
                sp.dma_start(p_dram[bass.ds(b, 1), :, :].rearrange("a c t -> (a c) t"), SELP).then_inc(s_p, 16)

            def load_weights(g):
                sp.dma_start(W1G[:, g % 2, :, :], w1[4 * g:4 * g + 4, 0:CH, :].rearrange("e d h -> d e h"))\
                    .then_inc(s_w[g % 2], 16)
                for q in range(4):
                    sp.dma_start(W2G[:, g % 2, q, :, :], w2[4 * g + q, 0:HID, :].rearrange("(c p) o -> p c o", p=128))\
                        .then_inc(s_w[g % 2], 16)

            sp.wait_ge(s_y2, BATCH * 16 + 16)
            sp.wait_ge(s_p, BATCH * 16 + 16)
            sp.wait_ge(s_pl, BATCH)
            for g in range(GRP):
                if g >= 2:
                    sp.wait_ge(s_wu, g - 1)
                load_weights(g)
            sp.wait_ge(s_oc, GRP)
            eo_v = eo_dram.rearrange("b (g q) o -> q b g o", q=4)
            for q in range(4):
                sp.dma_start(eo_v[q], ES[32 * q:32 * q + BATCH, :, :]).then_inc(s_eo, 16)
            sp.wait_ge(s_eo, 64)
            sp.dma_start(EO, eo_dram.rearrange("b e o -> e b o")).then_inc(s_eol, 16)
            for b in range(BATCH):
                i = b % 2
                if b >= 2:
                    sp.wait_ge(s_out[i], 16)
                sp.dma_start(YF[i], y2_dram[b]).then_inc(s_fl[i], 16)
                sp.dma_start(PF[i], p_dram[b]).then_inc(s_fl[i], 16)
                if b >= 1:
                    sp.wait_ge(s_fa, NCH * b)
                    sp.dma_start(out[b - 1], YF[1 - i]).then_inc(s_out[1 - i], 16)
            sp.wait_ge(s_fa, NCH * BATCH)
            sp.dma_start(out[BATCH - 1], YF[(BATCH - 1) % 2]).then_inc(s_out[(BATCH - 1) % 2], 16)
            sp.wait_ge(s_out[0], 32)
            sp.wait_ge(s_out[1], 32)

        @block.gpsimd
        def _(pool):
            pool.memset(ONES[:, :], 1.0).then_inc(s_ones, 1)
            pool.wait_ge(s_ones, 1)
            pool.memset(E2[HALF:HALF + 1, :], 1.0).then_inc(s_ones, 1)
            pool.sem_inc(s_wf[0], 1)
            pool.sem_inc(s_wf[1], 1)
            pool.sem_inc(s_pv, 2)
            pool.sem_inc(s_ps, 2)
            for s_one in (s_cc, s_pe, s_ac, s_cd, s_da, s_dd):
                pool.sem_inc(s_one, 1)
            pool.sem_inc(s_y2, 16)
            pool.sem_inc(s_p, 16)
            pool.sem_inc(s_tu, UNITS)
            pool.sem_inc(s_ep, 4)
            pool.sem_inc(s_es, 2)
            with pool.Fori(0, BATCH) as b:
                with pool.Fori(0, NCH) as c:
                    for q in range(NCH):
                        step = b * NCH * NCH + c * NCH + q
                        pool.wait_ge(s_pe, step + 2)
                        if q == 0:
                            wait_alone(pool, s_cc, b * NCH + c + 1)
                            pool.tensor_copy(PSUMS, PROB[:, 0]).then_inc(s_ps, 1)
                        else:
                            pool.wait_ge(s_ps, step + 2)
                            pool.tensor_tensor(PSUMS, PSUMS, PROB[:, q % 2], ALU.add).then_inc(s_ps, 1)

                pool.wait_ge(s_kr, b + 1)
                pool.wait_ge(s_xt, 2 * b * NBLK + NBLK)

                def step(cur, prev):
                    if cur is not None:
                        n = b * NB + cur.n
                        wait_alone(pool, s_ep, n + 1)
                        pool.tensor_copy(BR[:, cur.ring, :], B[:, bass.ds(cur.jb * 16, 16)]).then_inc(s_br, 1)
                        pool.tensor_copy(XR[:, cur.ring, :],
                                         XT[:, bass.ds(cur.jb, 1), :].rearrange("p a c -> p (a c)")).then_inc(s_xr, 1)
                    if prev is not None:
                        m = b * NB + prev.n
                        if prev.diag is None:
                            pool.wait_ge(s_ex, m + 1)
                        else:
                            pool.wait_ge(s_mk, b * NBLK + PER * prev.c + prev.diag + 1)
                        w = CHUNK - prev.off
                        dst = DS[:, prev.c % 2, prev.off:CHUNK]
                        if prev.first:
                            wait_alone(pool, s_es, m + 2)
                            pool.tensor_copy(dst, EB[:, prev.par, 0:w]).then_inc(s_es, 1)
                        else:
                            pool.wait_ge(s_es, m + 2)
                            pool.tensor_tensor(dst, dst, EB[:, prev.par, 0:w], ALU.add).then_inc(s_es, 1)

                each_block(pool, step)

        @block.scalar
        def _(act):
            with act.Fori(0, BATCH) as b:
                act.wait_ge(s_var, 3 * b + 1)
                nc.scalar.activation(SM[:, 4:5], SM[:, 3:4], ACT.Sqrt).then_inc(s_sd, 1)
                for ch in range(NCH):
                    t = slice(CHUNK * ch, CHUNK * ch + CHUNK)
                    act.wait_ge(s_ec, b * NCH + ch + 1)
                    nc.scalar.copy(E1P[0:HALF, t], E1[0:HALF, t])
                    nc.scalar.copy(E2H[0:HALF, t], E2[0:HALF, t])
                    nc.scalar.copy(E2H[HALF:, t], E2[0:HALF, t]).then_inc(s_eh, 1)
                with act.Fori(0, NCH) as c:
                    for q in range(NCH):
                        step = b * NCH * NCH + c * NCH + q
                        act.wait_ge(s_qk, step + 1)
                        act.wait_ge(s_pv, step + 1)
                        act.wait_ge(s_ps, step + 1)
                        nc.scalar.activation(PROB[:, q % 2], PS[:, 0:4, :], ACT.Exp).then_inc(s_pe, 1)
                act.wait_ge(s_var, 3 * b + 2)
                nc.scalar.activation(RS[:, :], RS[:, :], ACT.Sqrt).then_inc(s_sd, 1)
                for ch in range(NCH):
                    bank_ready(act, b, W_C + ch)
                    nc.scalar.copy(XN[:, CHUNK * ch:CHUNK * ch + CHUNK], bank(W_C + ch)).then_inc(s_wf[(W_C + ch) % 2], 1)
                for ch in range(NCH):
                    bank_ready(act, b, W_F + ch)
                    nc.scalar.activation(F[:, CHUNK * ch:CHUNK * ch + CHUNK], bank(W_F + ch), ACT.Identity,
                                         bias=pk("b1")).then_inc(s_wf[(W_F + ch) % 2], 1)
                bank_ready(act, b, W_B)
                nc.scalar.copy(B[:, :], bank(W_B)).then_inc(s_wf[W_B % 2], 1)

                def finish(prev):
                    m = b * NB + prev.n
                    w = CHUNK - prev.off
                    act.wait_ge(s_tu, UNITS * m + 2 * UNITS)
                    act.wait_ge(s_ep, m + 3)
                    act.wait_ge(s_es, m + 1)
                    nc.scalar.activation(EB[:, prev.par, 0:w], PS[:, prev.par, 0:w], ACT.Exp,
                                         bias=pk("b2")).then_inc(s_ex, 1)

                def step(cur, prev):
                    for k in range(UNITS if cur is not None else 0):
                        n = b * NB + cur.n
                        w = CHUNK - cur.off
                        act.wait_ge(s_sum, UNITS * n + k + 1)
                        nc.scalar.activation(S[:, k, :, 0:w], S[:, k, :, 0:w], ACT.Tanh).then_inc(s_th, 1)
                        if k == 1 and prev is not None:
                            finish(prev)
                    if cur is None:
                        finish(prev)

                each_block(act, step)

                act.wait_ge(s_var, 3 * b + 3)
                nc.scalar.activation(RS[:, :], RS[:, :], ACT.Sqrt).then_inc(s_sd, 1)
                for ch in range(NCH):
                    bank_ready(act, b, W_C2 + ch)
                    nc.scalar.copy(XN[:, CHUNK * ch:CHUNK * ch + CHUNK], bank(W_C2 + ch)).then_inc(s_wf[(W_C2 + ch) % 2], 1)
                act.wait_ge(s_lx, b + 1)
                nc.scalar.activation(LOG, LOG, ACT.Exp, bias=SM[0:EXP, 5:6], accum_out=SM[0:EXP, 6:7]).then_inc(s_le, 1)
            for g in range(GRP):
                act.wait_ge(s_h, g + 1)
                if g >= 1:
                    act.wait_ge(s_ht, g)
                nc.scalar.activation(HS, PS[:, g % 2, :], ACT.Gelu).then_inc(s_g, 1)

        @block.tensor
        def _(pe):
            mm = nc.tensor.matmul
            pe.wait_ge(s_const, 64)
            pe.wait_ge(s_ones, 2)

            def transposes(b, ch, k, src):
                bank_free(pe, b, k)
                for u in range(PER):
                    last = nc.tensor.transpose(bank(k)[:, BLK * u:BLK * u + BLK], src(PER * ch + u), pk("ident"))
                last.then_inc(s_wr[k % 2], 1)

            with pe.Fori(0, BATCH) as b:
                pe.wait_ge(s_chst, b + 1)
                bank_free(pe, b, W_GN)
                mm(bank(W_GN)[:, 0:1], pk("gmat"), MV[:, 0, 0:1], start=True, stop=True).then_inc(s_wr[W_GN % 2], 1)
                pe.wait_ge(s_chsq, b + 1)
                bank_free(pe, b, W_GN + 1)
                mm(bank(W_GN + 1)[:, 0:1], pk("gmat"), SM[:, 2:3], start=True, stop=True).then_inc(s_wr[(W_GN + 1) % 2], 1)
                pe.wait_ge(s_xn, b + 1)
                for ch in range(NCH):
                    k = W_E + 2 * ch
                    bank_free(pe, b, k)
                    mm(bank(k), pk("w12"), XN[:, CHUNK * ch:CHUNK * ch + CHUNK], start=True, stop=True).then_inc(s_wr[k % 2], 1)
                    bank_free(pe, b, k + 1)
                    for u in range(PER):
                        t = CHUNK * ch + BLK * u
                        last = mm(bank(k + 1)[:, BLK * u:BLK * u + BLK], XN[:, t:t + BLK], pk("wa"), start=True, stop=True)
                    last.then_inc(s_wr[(k + 1) % 2], 1)
                wait_alone(pe, s_e12, b + 1)
                with pe.Fori(0, 4) as h:
                    for ib in range(NBLK):
                        step = (b * 4 + h) * NBLK + ib
                        if ib >= 2:
                            wait_alone(pe, s_mxd, step - 1)
                        for u in range(2):
                            for e2 in (E2H, E2M):
                                last = mm(PS[:, 2 * (ib % 2) + u, :], E1P[:, BLK * ib:BLK * ib + BLK],
                                          e2[:, bass.ds(h * 1024 + 512 * u, 512)], start=(e2 is E2H), stop=(e2 is E2M))
                        last.then_inc(s_mxq, 1)
                    wait_alone(pe, s_mxd, (b * 4 + h + 1) * NBLK)
                pe.wait_ge(s_m1, b + 1)
                bank_free(pe, b, W_M)
                nc.tensor.transpose(bank(W_M)[0:NBLK, 0:128], M1[:, :], pk("ident")).then_inc(s_wr[W_M % 2], 1)
                pe.wait_ge(s_nmr, 16 * (b + 1))

                def scores(c, q):
                    pe.wait_ge(s_pe, b * NCH * NCH + c * NCH + q + 1)
                    for u in range(PER):
                        t = CHUNK * q + BLK * u
                        last = mm(PS[:, u, :], E2[:, t:t + BLK], E1[:, bass.ds(c * CHUNK, CHUNK)], start=True, stop=True)
                    last.then_inc(s_qk, 1)

                def values(c, q):
                    pe.wait_ge(s_pe, b * NCH * NCH + c * NCH + q + 2)
                    if q == 0:
                        pe.wait_ge(s_ac, b * NCH + c + 1)
                    for u in range(PER):
                        last = mm(ACC, VT[:, PER * q + u, :], PROB[:, q % 2, u, :],
                                  start=(q == 0 and u == 0), stop=(q == NCH - 1 and u == PER - 1))
                    last.then_inc(s_pv, 1)

                def chunk_end(c):
                    pe.wait_ge(s_ps, (b * NCH + c + 1) * NCH + 2)
                    pe.wait_ge(s_cd, b * NCH + c + 1)
                    for u in range(PER):
                        last = mm(DEN, ONES[:, :], PSUMS[:, u, :], start=(u == 0), stop=(u == PER - 1))
                    last.then_inc(s_cc, 1)

                scores(0, 0)
                with pe.Fori(0, NCH - 1) as c:
                    for q in range(NCH):
                        scores(c + (q + 1) // NCH, (q + 1) % NCH)
                        values(c, q)
                    chunk_end(c)
                for q in range(NCH):
                    if q + 1 < NCH:
                        scores(NCH - 1, q + 1)
                    values(NCH - 1, q)
                chunk_end(NCH - 1)

                pe.wait_ge(s_cx, NCH * (b + 1))
                for ch in range(NCH):
                    transposes(b, ch, W_T + ch, lambda i: X[:, BLK * i:BLK * i + BLK])
                for ch in range(NCH):
                    pe.wait_ge(s_xt, 2 * b * NBLK + PER * (ch + 1))
                    transposes(b, ch, W_C + ch, lambda i: XT[:, i, :])
                for ch in range(NCH):
                    bank_free(pe, b, W_F + ch)
                    if ch == 0:
                        bank_free(pe, b, W_F + 1)
                    mm(bank(W_F + ch), pk("w1a"), XN[:, CHUNK * ch:CHUNK * ch + CHUNK], start=True, stop=True)\
                        .then_inc(s_wr[(W_F + ch) % 2], 1)
                bank_free(pe, b, W_B)
                for r in range(KEYS):
                    last = mm(bank(W_B), w1b[:, r, :], XN[:, r:TOK:KEYS], start=(r == 0), stop=(r == KEYS - 1))
                last.then_inc(s_wr[W_B % 2], 1)

                def finish(prev):
                    m = b * NB + prev.n
                    w = CHUNK - prev.off
                    if prev.diag is None:
                        pe.wait_ge(s_ex, m + 1)
                    else:
                        pe.wait_ge(s_mk, b * NBLK + PER * prev.c + prev.diag + 1)
                    pe.wait_ge(s_xr, m + 1)
                    if prev.first:
                        pe.wait_ge(s_da, b * NCH + prev.c + 1)
                    mm(ACC[:, prev.off:CHUNK], XR[:, prev.ring, :], EB[:, prev.par, 0:w],
                       start=prev.first, stop=True, skip_group_check=True).then_inc(s_ep, 1)
                    if prev.last:
                        pe.wait_ge(s_es, m + 3)
                        pe.wait_ge(s_dd, b * NCH + prev.c + 1)
                        mm(DEN, ONES[:, :], DS[:, prev.c % 2, :], start=True, stop=True).then_inc(s_dc, 1)

                def step(cur, prev):
                    if cur is not None:
                        n = b * NB + cur.n
                        w = CHUNK - cur.off
                        for k in range(UNITS):
                            pe.wait_ge(s_th, UNITS * n + k + 1)
                            for q in range(4):
                                last = mm(PS[32 * q:32 * q + 32, cur.par, 0:w], w2k[:, k, :], S[:, k, q, 0:w],
                                          start=(k == 0), stop=(k == UNITS - 1))
                            last.then_inc(s_tu, 1)
                            if k == 2 and prev is not None:
                                finish(prev)
                    else:
                        finish(prev)

                each_block(pe, step)

                pe.wait_ge(s_dx, NCH * (b + 1))
                for ch in range(NCH):
                    transposes(b, ch, W_T2 + ch, lambda i: X[:, BLK * i:BLK * i + BLK])
                for ch in range(NCH):
                    pe.wait_ge(s_xt, (2 * b + 1) * NBLK + PER * (ch + 1))
                    transposes(b, ch, W_C2 + ch, lambda i: XT[:, i, :])
                for ch in range(NCH):
                    bank_free(pe, b, W_L + ch)
                    if ch == 0:
                        bank_free(pe, b, W_L + 1)
                    mm(bank(W_L + ch)[0:EXP, :], pk("gw"), XN[:, CHUNK * ch:CHUNK * ch + CHUNK], start=True, stop=True)\
                        .then_inc(s_wr[(W_L + ch) % 2], 1)
                pe.wait_ge(s_sp, b + 1)
                for t in range(4):
                    k = W_P + t
                    wait_alone(pe, s_wf[k % 2], b * UPB[k % 2] + uses_before(k) + 1)
                    for u in range(8):
                        i = 8 * t + u
                        last = nc.tensor.transpose(bank(k)[:, EXP * u:EXP * u + EXP], SELP[:, BLK * i:BLK * i + BLK],
                                                   pk("ident", EXP)[:, 0:EXP])
                    last.then_inc(s_wr[k % 2], 1)
                pe.wait_ge(s_pt, 4 * (b + 1))
                bank_free(pe, b, W_PL)
                for i in range(NBLK):
                    last = mm(bank(W_PL)[:, 0:EXP], XT[:, i, :], PT[:, i, :], start=(i == 0), stop=(i == NBLK - 1))
                last.then_inc(s_wr[W_PL % 2], 1)

            pe.wait_ge(s_pl, BATCH)

            def up(g):
                pe.wait_ge(s_w[g % 2], 80 * (g // 2 + 1))
                if g >= 2:
                    pe.wait_ge(s_g, g - 1)
                mm(PS[:, g % 2, :], SELB[:, 128 * g:128 * g + 128], B1A[:, :], start=True, stop=True, skip_group_check=True)
                for q in range(4):
                    last = mm(PS[32 * q:32 * q + BATCH, g % 2, :], PL[:, 4 * g + q, :], W1G[:, g % 2, q, :],
                              start=False, stop=True, skip_group_check=True)
                last.then_inc(s_h, 1)

            def down(g):
                pe.wait_ge(s_g, g + 1)
                if g >= 1:
                    pe.wait_ge(s_htc, g)
                for c in range(4):
                    last = nc.tensor.transpose(PS[:, 2, BLK * c:BLK * c + BLK], HS[:, BLK * c:BLK * c + BLK], pk("ident"))
                last.then_inc(s_ht, 1)
                pe.wait_ge(s_htc, g + 1)
                if g >= 2:
                    pe.wait_ge(s_oc, g - 1)
                mm(PS[:, 4 + g % 2, 0:OUT], SELB[:, 128 * g:128 * g + 128], B2A[:, :], start=True, stop=True, skip_group_check=True)
                for c in range(4):
                    for q in range(4):
                        last = mm(PS[32 * q:32 * q + BATCH, 4 + g % 2, 0:OUT], HT[:, c, 32 * q:32 * q + BATCH],
                                  W2G[:, g % 2, q, c, :], start=False, stop=True, skip_group_check=True)
                last.then_inc(s_wu, 1)

            up(0)
            for g in range(GRP):
                if g + 1 < GRP:
                    up(g + 1)
                down(g)
            pe.wait_ge(s_eol, 16)
            for b in range(BATCH):
                pe.wait_ge(s_fl[b % 2], 32 * (b // 2 + 1))
                for ch in range(NCH):
                    i = NCH * b + ch
                    if i >= 2:
                        pe.wait_ge(s_fa, i - 1)
                    mm(PS[:, i % 2, :], EO[:, b, :], PF[b % 2][:, CHUNK * ch:CHUNK * ch + CHUNK], start=True, stop=True)\
                        .then_inc(s_fm, 1)

        @block.vector
        def _(dve):
            v = nc.vector
            at = [0]
            VSTEPS = 83

            with dve.Fori(0, BATCH) as b:
                def link(ins, alone=False):
                    at[0] += 1
                    ins.then_inc(s_v, 1)
                    if alone:
                        wait_alone(dve, s_v, b * VSTEPS + at[0])
                    else:
                        dve.wait_ge(s_v, b * VSTEPS + at[0])

                dve.wait_ge(s_x, 16 * (b + 1))
                for ch in range(NCH):
                    last = v.bn_stats(ST[:, ch, :], X[:, CHUNK * ch:CHUNK * ch + CHUNK])
                link(last, alone=True)
                v.bn_aggr(MV[:, 0, :], ST[:, 0:NCH, :]).then_inc(s_chst, 1)
                bank_ready(dve, b, W_GN)
                v.tensor_copy(SM[:, 0:1], bank(W_GN)[:, 0:1]).then_inc(s_wf[W_GN % 2], 1)
                bank_free(dve, b, W_GN + 2)
                link(v.tensor_tensor(SM[:, 1:2], MV[:, 0, 0:1], SM[:, 0:1], ALU.subtract))
                v.scalar_tensor_tensor(SM[:, 2:3], SM[:, 1:2], SM[:, 1:2], MV[:, 0, 1:2], ALU.mult, ALU.add).then_inc(s_chsq, 1)
                bank_ready(dve, b, W_GN + 1)
                link(v.tensor_copy(SM[:, 7:8], bank(W_GN + 1)[:, 0:1]))
                v.tensor_scalar(SM[:, 3:4], SM[:, 7:8], GN_EPS, None, ALU.add).then_inc(s_var, 1)
                dve.wait_ge(s_sd, 3 * b + 1)
                v.reciprocal(SM[:, 5:6], SM[:, 4:5]).then_inc(s_wf[(W_GN + 1) % 2], 1)
                bank_free(dve, b, W_GN + 3)
                v.tensor_scalar(XN[:, :], X[:, :], SM[:, 0:1], SM[:, 5:6], ALU.subtract, ALU.mult).then_inc(s_xn, 1)
                dve.wait_ge(s_const, 64)
                def middle_parts(ch):
                    t = slice(CHUNK * ch, CHUNK * ch + CHUNK)
                    dve.wait_ge(s_eh, b * NCH + ch + 1)
                    v.tensor_tensor(E1P[HALF:, t], E1[0:HALF, t], E1P[0:HALF, t], ALU.subtract)
                    v.tensor_tensor(E2M[0:HALF, t], E2[0:HALF, t], E2H[0:HALF, t], ALU.subtract)
                    return v.tensor_tensor(E2M[HALF:, t], E2[0:HALF, t], E2H[0:HALF, t], ALU.subtract)

                for ch in range(NCH):
                    k, t = W_E + 2 * ch, slice(CHUNK * ch, CHUNK * ch + CHUNK)
                    bank_ready(dve, b, k)
                    link(v.tensor_scalar(T1[:, :], bank(k), pk("b12"), 0.0, ALU.add, ALU.min))
                    v.tensor_scalar(T2[:, :], bank(k), pk("b12"), 0.0, ALU.add, ALU.max).then_inc(s_wf[k % 2], 1)
                    bank_free(dve, b, k + 2)
                    v.scalar_tensor_tensor(E1[0:HALF, t], T1[0:HALF, :], pk("a12")[0:HALF], T2[0:HALF, :], ALU.mult, ALU.add)
                    v.scalar_tensor_tensor(E2[0:HALF, t], T1[HALF:, :], pk("a12")[HALF:], T2[HALF:, :], ALU.mult, ALU.add)\
                        .then_inc(s_ec, 1)
                    dve.wait_ge(s_ec, b * NCH + ch + 1)
                    bank_ready(dve, b, k + 1)
                    y = bank(k + 1).rearrange("p (u c) -> p u c", u=PER)
                    t1, t2 = (z[:, :].rearrange("p (u c) -> p u c", u=PER) for z in (T1, T2))
                    v.tensor_tensor(t2, y, pk("ba")[:, None, :].to_broadcast([128, PER, 128]), ALU.add)\
                        .then_inc(s_wf[(k + 1) % 2], 1)
                    bank_free(dve, b, k + 3)
                    link(v.tensor_scalar(t1, t2, 0.0, pk("aa"), ALU.min, ALU.mult))
                    last = v.scalar_tensor_tensor(VT[:, PER * ch:PER * ch + PER, :], t2, 0.0, t1, ALU.max, ALU.add)
                    link(last)
                    if ch >= 1:
                        middle_parts(ch - 1)
                middle_parts(NCH - 1).then_inc(s_e12, 1)
                with dve.Fori(0, 4) as h:
                    for ib in range(NBLK):
                        dve.wait_ge(s_mxq, (b * 4 + h) * NBLK + ib + 1)
                        v.tensor_reduce(MX[:, ib, bass.ds(h, 1)], PS[:, 2 * (ib % 2):2 * (ib % 2) + 2, :]
                                        .rearrange("p u n -> p (u n)"), AXX, ALU.max).then_inc(s_mxd, 1)
                dve.wait_ge(s_mxd, (b + 1) * 4 * NBLK)
                v.tensor_reduce(M1[:, :], MX[:, :, :], AXX, ALU.max).then_inc(s_m1, 1)
                bank_ready(dve, b, W_M)
                link(v.tensor_scalar(NM[:, :], bank(W_M)[0:NBLK, 0:128], -1.0, None, ALU.mult))
                v.tensor_copy(SM[0:1, 15:16], SM[0:1, 5:6]).then_inc(s_nm, 1)
                v.tensor_copy(SM[0:1, 7:8], SM[0:1, 5:6]).then_inc(s_wf[W_M % 2], 1)

                with dve.Fori(0, NCH) as c:
                    done = b * NCH + c
                    dve.wait_ge(s_cc, done + 2)
                    v.tensor_copy(ACCS[:, :], ACC).then_inc(s_ac, 1)
                    v.reciprocal(RD[:, :], DEN).then_inc(s_cd, 1)
                    dve.wait_ge(s_ac, done + 2)
                    dve.wait_ge(s_cd, done + 2)
                    v.tensor_tensor(T1[:, :], ACCS[:, :], RD[:, :], ALU.mult).then_inc(s_cm, 1)
                    dve.wait_ge(s_cm, done + 1)
                    xc = X[:, bass.ds(c * CHUNK, CHUNK)]
                    v.tensor_tensor(xc, xc, T1[:, :], ALU.add).then_inc(s_cx, 1)
                dve.wait_ge(s_cx, (b + 1) * NCH)

                def layer_norm(W, j):
                    for ch in range(NCH):
                        bank_ready(dve, b, W + ch)
                        for u in range(PER):
                            last = v.bn_stats(ST[:, PER * ch + u, :], bank(W + ch)[:, BLK * u:BLK * u + BLK])
                        link(last)
                        v.tensor_copy(XT[:, PER * ch:PER * ch + PER, :],
                                      bank(W + ch).rearrange("p (u c) -> p u c", u=PER)).then_inc(s_wf[(W + ch) % 2], 1)
                        for u in range(PER):
                            last = v.bn_aggr(MV[:, PER * ch + u, :], ST[:, PER * ch + u, :])
                        link(last)
                    bank_free(dve, b, W + NCH)
                    bank_free(dve, b, W + NCH + 1)
                    v.tensor_scalar(RS[:, :], MV[:, :, 1], LN_EPS, None, ALU.add).then_inc(s_var, 1)
                    dve.wait_ge(s_sd, 3 * b + 2 + j)
                    link(v.reciprocal(RS[:, :], RS[:, :]))
                    for i in range(NBLK):
                        v.tensor_scalar(XT[:, i, :], XT[:, i, :], MV[:, i, 0:1], RS[:, i:i + 1], ALU.subtract, ALU.mult)\
                            .then_inc(s_xt, 1)

                layer_norm(W_T, 0)
                bank_free(dve, b, W_F + NCH)
                bank_free(dve, b, W_F + NCH + 1)
                bank_free(dve, b, W_B + 2)
                v.tensor_copy(SM[0:1, 7:8], SM[0:1, 5:6]).then_inc(s_kr, 1)

                def normalize(c):
                    done = b * NCH + c
                    dve.wait_ge(s_dc, done + 1)
                    v.tensor_copy(ACCS[:, :], ACC).then_inc(s_da, 1)
                    v.tensor_scalar(RD[:, :], DEN, DEN_EPS, None, ALU.add).then_inc(s_dd, 1)
                    dve.wait_ge(s_da, done + 2)
                    dve.wait_ge(s_dd, done + 2)
                    link(v.reciprocal(RD[:, :], RD[:, :]))
                    link(v.tensor_tensor(T1[:, :], ACCS[:, :], RD[:, :], ALU.mult))
                    xc = X[:, CHUNK * c:CHUNK * c + CHUNK]
                    v.tensor_tensor(xc, xc, T1[:, :], ALU.add).then_inc(s_dx, 1)

                def step(cur, prev):
                    if cur is not None:
                        n = b * NB + cur.n
                        w = CHUNK - cur.off
                        q0 = CHUNK * cur.c + cur.off
                        dve.wait_ge(s_br, n + 1)
                        for k in range(UNITS):
                            dve.wait_ge(s_tu, UNITS * n + k + 1)
                            for q in range(4):
                                last = v.tensor_scalar(S[:, k, q, 0:w], F[:, q0:q0 + w],
                                                       BR[:, cur.ring, 4 * q + k:4 * q + k + 1], None, ALU.add)
                            last.then_inc(s_sum, 1)
                    if prev is not None and prev.diag is not None:
                        dve.wait_ge(s_ex, b * NB + prev.n + 1)
                        e = EB[:, prev.par, 0:BLK]
                        v.tensor_tensor(e, e, pk("tri"), ALU.mult).then_inc(s_mk, 1)
                    if prev is not None and prev.last:
                        normalize(prev.c)

                each_block(dve, step)
                dve.wait_ge(s_dx, (b + 1) * NCH)
                layer_norm(W_T2, 1)

                for ch in range(NCH):
                    k = W_L + ch
                    bank_ready(dve, b, k)
                    v.tensor_scalar(LOG[:, CHUNK * ch:CHUNK * ch + CHUNK], bank(k)[0:EXP, :], pk("gb", EXP), None, ALU.add)\
                        .then_inc(s_wf[k % 2], 1)
                bank_free(dve, b, W_L + NCH)
                bank_free(dve, b, W_L + NCH + 1)
                link(v.tensor_reduce(SM[0:EXP, 4:5], LOG, AXX, ALU.max))
                v.tensor_scalar(SM[0:EXP, 5:6], SM[0:EXP, 4:5], -1.0, None, ALU.mult).then_inc(s_lx, 1)
                dve.wait_ge(s_le, b + 1)
                link(v.reciprocal(SM[0:EXP, 7:8], SM[0:EXP, 6:7]))
                link(v.tensor_scalar(LOG, LOG, SM[0:EXP, 7:8], None, ALU.mult), alone=True)
                link(v.max(TOP[:, :], LOG), alone=True)
                link(v.match_replace(REM, TOP[:, :], LOG, 0.0))
                v.tensor_tensor(SELP, LOG, REM, ALU.subtract).then_inc(s_sp, 1)
                for t in range(4):
                    bank_ready(dve, b, W_P + t)
                    v.tensor_copy(PT[:, 8 * t:8 * t + 8, :], bank(W_P + t).rearrange("p (k e) -> p k e", e=EXP))\
                        .then_inc(s_wf[(W_P + t) % 2], 1)
                bank_free(dve, b, W_P + 4)
                bank_free(dve, b, W_P + 5)
                v.tensor_copy(SM[0:1, 7:8], SM[0:1, 5:6]).then_inc(s_pt, 4)
                bank_ready(dve, b, W_PL)
                v.tensor_copy(PL[:, :, bass.ds(b, 1)], bank(W_PL)[:, 0:EXP][:, :, None]).then_inc(s_wf[W_PL % 2], 1)
                bank_free(dve, b, W_PL + 2)
                v.tensor_copy(SM[0:1, 7:8], SM[0:1, 5:6]).then_inc(s_pl, 1)
                assert at[0] == VSTEPS, at[0]

            for g in range(GRP):
                dve.wait_ge(s_ht, g + 1)
                if g >= 1:
                    dve.wait_ge(s_wu, g)
                v.tensor_copy(HT, PS[:, 2, :].rearrange("p (c m) -> p c m", c=4)).then_inc(s_htc, 1)
                dve.wait_ge(s_wu, g + 1)
                v.tensor_copy(ES[:, g, :], PS[:, 4 + g % 2, 0:OUT]).then_inc(s_oc, 1)
            for b in range(BATCH):
                for ch in range(NCH):
                    i = NCH * b + ch
                    dve.wait_ge(s_fm, i + 1)
                    yc = YF[b % 2][:, CHUNK * ch:CHUNK * ch + CHUNK]
                    v.tensor_tensor(yc, yc, PS[:, i % 2, :], ALU.add).then_inc(s_fa, 1)


def kernel(**inputs):
    import numpy as np
    import concourse.bacc as _bacc
    from concourse import mybir as _mybir
    from concourse.bass_utils import run_bass_kernel_spmd as _run

    a = {k: np.ascontiguousarray(v) for k, v in inputs.items()}
    pack = np.zeros((128, NPACK), np.float32)

    def put(name, value, rows=128):
        s, e = _AT[name]
        pack[0:rows, s:e] = value

    put("ident", np.eye(128, dtype=np.float32))
    put("gmat", np.kron(np.eye(32, dtype=np.float32), np.full((4, 4), 0.25, np.float32)))
    put("tri", np.triu(np.ones((128, 128), np.float32), 1))
    put("w12", np.concatenate([a["L0_conv_w1"].T, a["L0_conv_w2"].T], axis=1))
    put("wa", a["L0_conv_wa"].T)
    put("gw", a["L1_ffn_gate_w"].T)
    W1 = a["L1_attn_W1"]
    put("w1a", np.tile(W1[0:128], (1, 8)))
    w1b = np.zeros((128, 8, 8, 16), np.float32)
    w2k = np.zeros((8, 16, 4, 4, 8), np.float32)
    for r in range(8):
        w1b[:, r, r, :] = W1[128:256]
        for k in range(4):
            w2k[r, :, k, k, r] = a["L1_attn_w2"][:, 0]
    put("w1b", w1b.reshape(128, -1))
    put("w2k", w2k.reshape(128, -1))
    put("ba", np.broadcast_to(a["L0_conv_ba"], (128, 128)))
    put("b12", np.concatenate([a["L0_conv_b1"], a["L0_conv_b2"]])[:, None])
    put("a12", np.concatenate([np.broadcast_to(a["L0_conv_a1"], (64,)), np.broadcast_to(a["L0_conv_a2"], (64,))])[:, None])
    put("b1", np.tile(a["L1_attn_b1"], 8)[:, None])
    put("b2", np.broadcast_to(a["L1_attn_b2"], (128, 1)))
    put("aa", np.broadcast_to(a["L0_conv_aa"], (128, 1)))
    put("gb", a["L1_ffn_gate_b"][:, None], 64)
    arrays = {
        "x": a["x"].reshape(BATCH, CH, TOK),
        "pack": pack,
        "sel": np.repeat(np.eye(EXP, dtype=np.float32), 32, axis=1),
        "w1": a["L1_ffn_weight1"],
        "w2": a["L1_ffn_weight2"],
        "b1all": np.ascontiguousarray(a["L1_ffn_weight1"][:, CH, :]),
        "b2all": np.ascontiguousarray(a["L1_ffn_weight2"][:, HID, :]),
    }
    nc = _bacc.Bacc("TRN2", target_bir_lowering=False, num_devices=1)
    f32 = _mybir.dt.float32
    args = [nc.dram_tensor(f"in_{k}", v.shape, f32, kind="ExternalInput").ap() for k, v in arrays.items()]
    args.append(nc.dram_tensor("out_0", (BATCH, CH, TOK), f32, kind="ExternalOutput").ap())
    args.append(nc.dram_tensor("y2_scratch", (BATCH, CH, TOK), f32, kind="Internal").ap())
    args.append(nc.dram_tensor("p_scratch", (BATCH, EXP, TOK), f32, kind="Internal").ap())
    args.append(nc.dram_tensor("eo_scratch", (BATCH, EXP, OUT), f32, kind="Internal").ap())
    hybrid_kernel(nc, *args)
    r = _run(nc, [{f"in_{k}": v for k, v in arrays.items()}], core_ids=[0])
    return r.results[0]["out_0"].reshape(BATCH, CH, 64, 64)
```

```python
import concourse.bass as bass
from concourse import mybir
from contextlib import ExitStack

BATCH, CH, TOK = 4, 128, 4096
HALF = CH // 2
CHUNK = 512
NCH = TOK // CHUNK
BLK = 128
NBLK = TOK // BLK
PER = CHUNK // BLK
AH = 16
KEYS = CH // AH
UNITS = 4
EXP, HID, OUT = 64, 512, 128
GRP = EXP // 4
PAIR = 2
PPC = NBLK // PAIR
PAIRS = NCH * PPC
SKIP = 2
GN_EPS, LN_EPS, DEN_EPS = 1e-5, 1e-5, 1e-10

_COLS = [("ident", 128), ("gmat", 128), ("tri", 128), ("w12", 128), ("wa", 128), ("gw", 64), ("w1a", 128),
         ("w1b", 8 * 128), ("w2k", 4 * 32), ("ba", 128), ("b12", 1), ("a12", 1), ("b1", 1), ("b2", 1),
         ("aa", 1), ("gb", 1)]
_AT, _n = {}, 0
for _k, _w in _COLS:
    _AT[_k] = (_n, _n + _w)
    _n += _w
NPACK = _n


def blocks_before(c):
    return PER * c * (c + 1) // 2


NB = blocks_before(NCH)


class Block:

    def __init__(self, n, c, jb, diag, first, last):
        self.n, self.c, self.jb, self.diag, self.first, self.last = n, c, jb, diag, first, last
        self.off = 0 if diag is None else BLK * diag
        self.par = self.ring = None


def each_block(eng, emit):
    prev = None
    for c in range(NCH):
        n0, full = blocks_before(c), PER * c

        def blk(jb, ring, diag=None):
            x = Block(n0 + jb, c, jb, diag, isinstance(jb, int) and jb == 0, diag == PER - 1)
            x.par, x.ring = ring % 2, ring
            return x

        if full:
            for u in range(PER):
                cur = blk(u, u)
                emit(cur, prev)
                prev = cur
        if c > 1:
            with eng.Fori(1, c) as h:
                for u in range(PER):
                    cur = blk(PER * h + u, u)
                    emit(cur, blk(PER * h + u - 1, (u - 1) % PER))
            prev = blk(full - 1, PER - 1)
        for d in range(PER):
            cur = blk(full + d, d, d)
            emit(cur, prev)
            prev = cur
    emit(None, prev)


def hybrid_kernel(nc, x, pack, sel, wg, b1all, b2all, out, y2_dram, p_dram, eo_dram):
    f32, bf16 = mybir.dt.float32, mybir.dt.bfloat16
    ALU = mybir.AluOpType
    ACT = mybir.ActivationFunctionType
    AXX = mybir.AxisListType.X
    mm = nc.tensor.matmul
    ctx = ExitStack()
    with ctx:
        def sb(name, shape):
            return ctx.enter_context(nc.sbuf_tensor(name, shape, f32))

        def sem(name):
            return ctx.enter_context(nc.semaphore(name))

        PK = sb("packed", [128, NPACK])
        X = sb("residual", [128, TOK])
        XN = sb("normed_channels", [128, TOK])
        E1 = sb("e1_and_minus_max", [HALF + 1, TOK])
        E2 = sb("e2", [HALF, TOK])
        VT = sb("asm_tokens", [128, NBLK, 128])
        XT = sb("normed_tokens", [128, NBLK, 128])
        F = sb("query_part", [128, TOK])
        SA = sb("conv_prob_sums", [128, TOK])
        S = sb("tanh_slots", [128, UNITS, 4, CHUNK])
        PROB = sb("conv_probs", [128, 2, PAIR, CHUNK])
        E2R = sb("e2_and_ones_ring", [HALF + 1, PER, PAIR * BLK])
        VR = sb("asm_ring", [128, PER, PAIR * 128])
        EB = sb("exp_scores", [128, 2, CHUNK])
        DS = sb("exp_sums", [128, 2, CHUNK])
        ACCS = sb("context_copy", [128, CHUNK])
        RD = sb("recip_denominator", [128, CHUNK])
        B = sb("key_part", [128, TOK // KEYS])
        BR = sb("key_part_ring", [128, PER, CH // KEYS])
        XR = sb("value_ring", [128, PER, 128])
        ONES = sb("ones", [128, 128])
        M1 = sb("row_max_all", [128, NBLK])
        NM = sb("rows", [NBLK, 128])
        ST = sb("stats", [128, NBLK, 6])
        MV = sb("mean_var", [128, NBLK, 2])
        RS = sb("rstd", [128, NBLK])
        SM = sb("small", [128, 16])
        PL = sb("pooled", [128, EXP, BATCH])
        T1 = sb("tmp_low", [128, CHUNK])
        T2 = sb("tmp_high", [128, CHUNK])
        TOP = M1[0:EXP, 0:8]
        MX = T1[:, 0:4 * NBLK].rearrange("p (i h) -> p i h", h=4)
        flat = S[:, :, :, :].rearrange("p a b c -> p (a b c)")
        CA = XN[:, :]
        half = XN[:, :].bitcast(bf16)
        E1P, E2H = half[:, 0:TOK], half[:, TOK:2 * TOK]
        E2M = flat[:, 0:TOK // 2].bitcast(bf16)
        XC2 = VT[:, :, :].rearrange("p a b -> p (a b)")
        PT = flat[:, 0:NBLK * EXP].rearrange("p (k e) -> p k e", e=EXP)
        LOG, REM, SELP = E1[0:EXP, :], E2[0:EXP, :], F[0:EXP, :]
        WG = [SA[:, :], XN[:, :], flat[:, TOK:2 * TOK], flat[:, 0:TOK]]
        W1G = [w[:, 0:2048].rearrange("p (e h) -> p e h", e=4) for w in WG]
        W2G = [w[:, 2048:4096].rearrange("p (e c o) -> p e c o", e=4, c=4) for w in WG]
        SELB = XC2[0:EXP, 2048:4096]
        B1A = PROB[0:EXP, 0, 0, :]
        B2A = PROB[0:EXP, 0, 1, 0:OUT]
        HS = X[:, 0:HID]
        HT = X[:, 1024:1536].rearrange("p (c m) -> p c m", c=4)
        ES = VT[:, 0:GRP, :]
        EO = XT[0:EXP, 0:BATCH, :]
        YF = [F[:, :], flat[:, TOK:2 * TOK]]
        PF = [E1[0:EXP, :], E2[0:EXP, :]]
        PS = ctx.enter_context(nc.psum_tensor("ps", [128, 8, 512], f32))
        ACC, DEN, PVB = PS[:, 4, :], PS[:, 5, :], PS[:, 6, :]

        def pk(k, rows=128):
            a, z = _AT[k]
            return PK[0:rows, a:z]

        w1b = pk("w1b").rearrange("p (r m) -> p r m", r=KEYS)
        w2k = pk("w2k").rearrange("p (k m) -> p k m", k=4)

        s_const = sem("consts_loaded")
        s_ones = sem("ones_set")
        s_x = sem("x_to_norm_loaded")
        s_xr = sem("x_residual_loaded")
        s_y2 = sem("y2_saved")
        s_p = sem("probs_saved")
        s_alone = sem("waits_alone")
        s_v = sem("vector_step")
        s_chst = sem("channel_stats_ready")
        s_chsq = sem("channel_squares_ready")
        s_gv = sem("group_variance_ready")
        s_gd = sem("group_stddev_ready")
        s_lv = sem("token_variance_ready")
        s_ld = sem("token_stddev_ready")
        s_xn = sem("gn_ready")
        s_wr = [sem(f"work_bank_ready{i}") for i in range(2)]
        s_wf = [sem(f"work_bank_free{i}") for i in range(2)]
        s_ea = sem("projections_ready")
        s_eh = sem("e_high_parts_ready")
        s_em = sem("e_middle_parts_ready")
        s_mxq = sem("max_scores_ready")
        s_mxd = sem("max_scores_used")
        s_m1 = sem("row_max_ready")
        s_nm = sem("minus_max_ready")
        s_nmr = sem("minus_max_row_loaded")
        s_cz = sem("conv_sums_cleared")
        s_cr = sem("conv_rings_ready")
        s_qk = sem("conv_scores_ready")
        s_pe = sem("conv_probs_ready")
        s_pv = sem("conv_probs_used")
        s_pt1 = sem("conv_pair_summed")
        s_ps = sem("conv_sums_added")
        s_ca = sem("conv_numerator_added")
        s_rr = sem("recip_rows_ready")
        s_rrl = sem("recip_row_loaded")
        s_cm = sem("conv_scaled")
        s_cx = sem("conv_residual_added")
        s_xt = sem("tokens_ready")
        s_kr = sem("query_and_key_parts_ready")
        s_br = sem("key_parts_copied")
        s_vr = sem("value_ring_ready")
        s_sum = sem("sums_ready")
        s_th = sem("tanh_ready")
        s_tu = sem("tanh_used")
        s_ex = sem("exp_ready")
        s_mk = sem("exp_masked")
        s_ep = sem("exp_used_by_product")
        s_es = sem("exp_used_by_sum")
        s_dc = sem("context_chunk_ready")
        s_da = sem("context_copied")
        s_dd = sem("denominator_used")
        s_dx = sem("context_added")
        s_lx = sem("gate_max_ready")
        s_le = sem("gate_exp_ready")
        s_sp = sem("selected_ready")
        s_pt = sem("selected_tokens_ready")
        s_pl = sem("pooled_ready")
        s_ec = sem("expert_consts_loaded")
        s_w = [sem(f"ffn_weights_loaded{i}") for i in range(len(WG))]
        s_wu = sem("ffn_weights_used")
        s_h = sem("ffn_hidden_ready")
        s_g = sem("ffn_gelu_ready")
        s_ht = sem("ffn_hidden_transposed")
        s_htc = sem("ffn_hidden_copied")
        s_oc = sem("ffn_out_copied")
        s_eo = sem("expert_out_saved")
        s_eol = sem("expert_out_loaded")
        s_fl = [sem(f"final_inputs_loaded{i}") for i in range(2)]
        s_fm = sem("final_product_ready")
        s_fa = sem("final_added")
        s_out = [sem(f"out_saved{i}") for i in range(2)]

        SECTIONS = {
            "prep": [("gn", 2), ("e", 2 * NCH), ("max", 1)],
            "ln": [("t", NCH), ("c", NCH), ("f", NCH), ("b", 1)],
            "gate": [("t", NCH), ("c", NCH), ("l", NCH), ("p", 4), ("pl", 1)],
            "fin": [("den", 1), ("row", 1), ("bc", NCH)],
        }

        def uses(section, step, i):
            n = 0
            for name, count in SECTIONS[section]:
                if name == step:
                    break
                n += count + (count == 1 and name not in ("den", "row"))
            n += i
            lone, at = [], 0
            for name, count in SECTIONS[section]:
                at += count
                if count == 1 and name not in ("den", "row"):
                    lone.append(at)
                    at += 1
            return n % 2, sum(1 for k in range(n % 2, n, 2) if k not in lone)

        def total(*sections):
            return [sum(TOTALS[k][p] for k in sections) for p in range(2)]

        TOTALS = {}
        for k, steps in SECTIONS.items():
            TOTALS[k] = [0, 0]
            for name, count in steps:
                for i in range(count):
                    TOTALS[k][uses(k, name, i)[0]] += 1
        PRO, ITER = total("prep", "fin"), total("ln", "prep", "gate", "fin")

        def before(section, b, p):
            first = isinstance(b, int) and b == 0
            if section == "prep":
                return 0 if first else (b - 1) * ITER[p] + PRO[p] + total("ln")[p]
            if section == "fin":
                return total("prep")[p] if first else (b - 1) * ITER[p] + PRO[p] + total("ln", "prep", "gate")[p]
            n = b * ITER[p] + PRO[p]
            if section == "gate":
                last = isinstance(b, int) and b == BATCH - 1
                n = n + (total("ln") if last else total("ln", "prep"))[p]
            return n

        def bank(section, step, i=0):
            return PS[:, 6 + uses(section, step, i)[0], :]

        def used(section, step, i=0):
            return s_wf[uses(section, step, i)[0]]

        def written(section, step, i=0):
            return s_wr[uses(section, step, i)[0]]

        def bank_ready(eng, section, b, step, i=0):
            p, n = uses(section, step, i)
            eng.wait_ge(s_wr[p], before(section, b, p) + n + 1)

        def bank_free(eng, section, b, step, i=0, alone=False):
            p, n = uses(section, step, i)
            (wait_alone if alone else wait)(eng, s_wf[p], before(section, b, p) + n + 1)

        def bank_read(eng, section, b, step, i=0):
            p, n = uses(section, step, i)
            eng.wait_ge(s_wf[p], before(section, b, p) + n + 2)

        def wait(eng, sm, value):
            eng.wait_ge(sm, value)

        def wait_alone(eng, sm, value):
            eng.wait_ge(sm, value)
            eng.sem_inc(s_alone, 1)

        def schedule(eng, prep, conv_alone, finalize, norm, attend, gate):
            prep(0)
            conv_alone()
            finalize(0)
            with eng.Fori(0, BATCH - 1) as b:
                norm(b)
                prep(b + 1)
                attend(b, True)
                gate(b)
                finalize(b + 1)
            norm(BATCH - 1)
            attend(BATCH - 1, False)
            gate(BATCH - 1)

        def beside(cur):
            if cur is None or cur.c < SKIP or (cur.c == NCH - 1 and cur.diag is not None):
                return None
            return cur.n - blocks_before(SKIP)

        def alone_pairs(eng, emit):
            for u in range(PER):
                emit(u, u, u == 0)
            with eng.Fori(1, PAIRS // PER) as h:
                for u in range(PER):
                    emit(PER * h + u, u, False)

        def cols(p):
            if isinstance(p, int):
                return p // PPC * CHUNK, p % PPC * (PAIR * BLK)
            return (p // PPC) * CHUNK, (p % PPC) * (PAIR * BLK)

        block = ctx.enter_context(nc.Block())

        @block.sync
        def _(sp):
            sp.dma_start(PK[:, :], pack).then_inc(s_const, 16)

            def prep(b):
                if not isinstance(b, int):
                    wait_alone(sp, s_kr, b)
                sp.dma_start(XN[:, :], rows(x, b)).then_inc(s_x, 16)
                sp.wait_ge(s_nm, b + 1)
                sp.dma_start(E1[HALF:HALF + 1, :], NM[:, :]).then_inc(s_nmr, 16)

            def rows(dram, b):
                return dram[b] if isinstance(b, int) else dram[bass.ds(b, 1), :, :].rearrange("a c t -> (a c) t")

            def conv_alone():
                pass

            def finalize(b):
                if not isinstance(b, int):
                    wait_alone(sp, s_y2, 16 * b)
                    wait_alone(sp, s_lv, 2 * b)
                sp.dma_start(X[:, :], rows(x, b)).then_inc(s_xr, 16)
                sp.wait_ge(s_rr, b + 1)
                sp.dma_start(E1[HALF:HALF + 1, :], NM[:, :]).then_inc(s_rrl, 16)

            def norm(b):
                pass

            def attend(b, conv):
                wait_alone(sp, s_dx, (b + 1) * NCH)
                sp.dma_start(rows(y2_dram, b), X[:, :]).then_inc(s_y2, 16)

            def gate(b):
                wait_alone(sp, s_sp, b + 1)
                sp.dma_start(rows(p_dram, b), SELP).then_inc(s_p, 16)

            def load_experts(g):
                sp.dma_start(WG[g % len(WG)], wg[g]).then_inc(s_w[g % len(WG)], 16)

            def attend_last(b, conv):
                if not conv:
                    sp.wait_ge(s_cx, NCH * BATCH)
                    sp.wait_ge(s_kr, BATCH)
                    load_experts(0)
                    load_experts(1)
                attend(b, conv)
                if not conv:
                    load_experts(2)

            schedule(sp, prep, conv_alone, finalize, norm, attend_last, gate)
            sp.wait_ge(s_pl, BATCH)
            sp.dma_start(SELB, sel).then_inc(s_ec, 16)
            sp.dma_start(B1A, b1all).then_inc(s_ec, 16)
            sp.dma_start(B2A, b2all).then_inc(s_ec, 16)

            def load_final(b):
                sp.dma_start(YF[b % 2], y2_dram[b]).then_inc(s_fl[b % 2], 16)
                sp.dma_start(PF[b % 2], p_dram[b]).then_inc(s_fl[b % 2], 16)

            for g in range(3, GRP):
                if g >= len(WG):
                    sp.wait_ge(s_wu, g - len(WG) + 1)
                load_experts(g)
            sp.wait_ge(s_y2, BATCH * 16)
            sp.wait_ge(s_p, BATCH * 16)
            load_final(0)
            sp.wait_ge(s_wu, GRP - 1)
            load_final(1)
            sp.wait_ge(s_oc, GRP)
            eo_v = eo_dram.rearrange("b (g q) o -> q b g o", q=4)
            for q in range(4):
                sp.dma_start(eo_v[q], ES[32 * q:32 * q + BATCH, :, :]).then_inc(s_eo, 16)
            sp.wait_ge(s_eo, 64)
            sp.dma_start(EO, eo_dram.rearrange("b e o -> e b o")).then_inc(s_eol, 16)
            for b in range(1, BATCH):
                sp.wait_ge(s_fa, NCH * b)
                sp.dma_start(out[b - 1], YF[(b - 1) % 2]).then_inc(s_out[(b - 1) % 2], 16)
                if b + 1 < BATCH:
                    sp.wait_ge(s_out[(b + 1) % 2], 16)
                    load_final(b + 1)
            sp.wait_ge(s_fa, NCH * BATCH)
            sp.dma_start(out[BATCH - 1], YF[(BATCH - 1) % 2]).then_inc(s_out[(BATCH - 1) % 2], 16)
            sp.wait_ge(s_out[0], 32)
            sp.wait_ge(s_out[1], 32)

        @block.gpsimd
        def _(pool):
            pool.memset(ONES[:, :], 1.0).then_inc(s_ones, 1)
            pool.wait_ge(s_ones, 1)
            pool.memset(E2R[HALF:HALF + 1, :, :], 1.0).then_inc(s_ones, 1)
            pool.sem_inc(s_wf[0], 1)
            pool.sem_inc(s_wf[1], 1)
            pool.sem_inc(s_pv, 4)
            pool.sem_inc(s_ps, 2)
            pool.sem_inc(s_mxd, 4)
            for s_one in (s_pe, s_ca, s_da, s_dd, s_sum):
                pool.sem_inc(s_one, 1)
            pool.sem_inc(s_tu, UNITS)
            pool.sem_inc(s_ep, 4)
            pool.sem_inc(s_es, 2)

            def prep(b):
                if isinstance(b, int) and b == 0:
                    pool.wait_ge(s_ones, 2)
                else:
                    wait_alone(pool, s_cx, b * NCH)
                pool.memset(SA[:, :], 0.0).then_inc(s_cz, 1)
                wait_alone(pool, s_m1, b + 1)
                wait_alone(pool, s_cz, 2 * b + 1)
                pool.memset(CA, 0.0).then_inc(s_cz, 1)
                pool.wait_ge(s_cz, 2 * b + 2)

            def conv_sum(b, p, slot):
                pool.wait_ge(s_pe, b * PAIRS + p + 2)
                pool.wait_ge(s_ps, b * PAIRS + p + 2)
                pool.tensor_tensor(T2[:, :], PROB[:, slot % 2, 0, :], PROB[:, slot % 2, 1, :], ALU.add).then_inc(s_pt1, 1)
                pool.wait_ge(s_pt1, b * PAIRS + p + 1)
                sc = SA[:, bass.ds(cols(p)[0], CHUNK)]
                pool.tensor_tensor(sc, sc, T2[:, :], ALU.add).then_inc(s_ps, 1)

            def conv_alone():
                def pair(p, slot, first):
                    if not first:
                        conv_sum(0, p - 1, (slot - 1) % PER)

                alone_pairs(pool, pair)
                conv_sum(0, PAIRS - 1, 3)

            def finalize(b):
                pass

            def norm(b):
                pass

            def attend(b, conv):
                pool.wait_ge(s_kr, b + 1)

                def step(cur, prev):
                    if cur is not None:
                        n = b * NB + cur.n
                        wait_alone(pool, s_ep, n + 1)
                        pool.tensor_copy(XR[:, cur.ring, :],
                                         XT[:, bass.ds(cur.jb, 1), :].rearrange("p a c -> p (a c)")).then_inc(s_vr, 1)
                    if prev is not None:
                        m = b * NB + prev.n
                        if prev.diag is None:
                            pool.wait_ge(s_ex, m + 1)
                        else:
                            pool.wait_ge(s_mk, b * NBLK + PER * prev.c + prev.diag + 1)
                        w = CHUNK - prev.off
                        dst = DS[:, prev.c % 2, prev.off:CHUNK]
                        if prev.first:
                            wait_alone(pool, s_es, m + 2)
                            pool.tensor_copy(dst, EB[:, prev.par, 0:w]).then_inc(s_es, 1)
                        else:
                            pool.wait_ge(s_es, m + 2)
                            pool.tensor_tensor(dst, dst, EB[:, prev.par, 0:w], ALU.add).then_inc(s_es, 1)
                        q = beside(prev) if conv else None
                        if q is not None:
                            conv_sum(b + 1, q, prev.ring)

                each_block(pool, step)

            def gate(b):
                pass

            schedule(pool, prep, conv_alone, finalize, norm, attend, gate)

        @block.scalar
        def _(act):
            def conv_exp(b, p, slot, banks):
                act.wait_ge(s_qk, b * PAIRS + p + 1)
                act.wait_ge(s_pv, b * PAIRS + p + 3)
                act.wait_ge(s_ps, b * PAIRS + p + 1)
                nc.scalar.activation(PROB[:, slot % 2], PS[:, banks:banks + PAIR, :], ACT.Exp).then_inc(s_pe, 1)

            def prep(b):
                act.wait_ge(s_gv, b + 1)
                nc.scalar.activation(SM[:, 4:5], SM[:, 3:4], ACT.Sqrt).then_inc(s_gd, 1)
                act.wait_ge(s_ea, b + 1)
                nc.scalar.copy(E1P[0:HALF, :], E1[0:HALF, :]).then_inc(s_eh, 1)
                nc.scalar.copy(E2H[0:HALF, :], E2[:, :]).then_inc(s_eh, 1)
                nc.scalar.copy(E2H[HALF:, :], E2[:, :]).then_inc(s_eh, 1)

            def conv_alone():
                alone_pairs(act, lambda p, slot, first: conv_exp(0, p, slot, 2 - 2 * (slot % 2)))

            def finalize(b):
                pass

            def layer_norm(section, b, j, dst):
                act.wait_ge(s_lv, 2 * b + 1 + j)
                nc.scalar.activation(RS[:, :], RS[:, :], ACT.Sqrt).then_inc(s_ld, 1)
                for ch in range(NCH):
                    bank_ready(act, section, b, "c", ch)
                    nc.scalar.copy(dst[:, CHUNK * ch:CHUNK * ch + CHUNK], bank(section, "c", ch)).then_inc(used(section, "c", ch), 1)

            def norm(b):
                layer_norm("ln", b, 0, XN)
                for ch in range(NCH):
                    bank_ready(act, "ln", b, "f", ch)
                    nc.scalar.activation(F[:, CHUNK * ch:CHUNK * ch + CHUNK], bank("ln", "f", ch), ACT.Identity,
                                         bias=pk("b1")).then_inc(used("ln", "f", ch), 1)
                bank_ready(act, "ln", b, "b")
                nc.scalar.copy(B[:, :], bank("ln", "b")).then_inc(used("ln", "b"), 1)

            def attend(b, conv):
                def finish(prev):
                    m = b * NB + prev.n
                    w = CHUNK - prev.off
                    act.wait_ge(s_tu, UNITS * m + 2 * UNITS)
                    act.wait_ge(s_ep, m + 3)
                    act.wait_ge(s_es, m + 1)
                    nc.scalar.activation(EB[:, prev.par, 0:w], PS[:, prev.par, 0:w], ACT.Exp,
                                         bias=pk("b2")).then_inc(s_ex, 1)

                def step(cur, prev):
                    for k in range(UNITS if cur is not None else 0):
                        n = b * NB + cur.n
                        w = CHUNK - cur.off
                        act.wait_ge(s_sum, UNITS * n + k + 2)
                        nc.scalar.activation(S[:, k, :, 0:w], S[:, k, :, 0:w], ACT.Tanh).then_inc(s_th, 1)
                        if k == 1 and prev is not None:
                            finish(prev)
                    if cur is None:
                        finish(prev)
                    p = beside(cur) if conv else None
                    if p is not None:
                        conv_exp(b + 1, p, cur.ring, 2)

                each_block(act, step)

            def gate(b):
                layer_norm("gate", b, 1, XC2)
                act.wait_ge(s_lx, b + 1)
                nc.scalar.activation(LOG, LOG, ACT.Exp, bias=SM[0:EXP, 5:6], accum_out=SM[0:EXP, 6:7]).then_inc(s_le, 1)

            schedule(act, prep, conv_alone, finalize, norm, attend, gate)
            for g in range(GRP):
                act.wait_ge(s_h, g + 1)
                if g >= 1:
                    act.wait_ge(s_ht, g)
                nc.scalar.activation(HS, PS[:, g % 2, :], ACT.Gelu).then_inc(s_g, 1)

        @block.tensor
        def _(pe):
            pe.wait_ge(s_const, 16)
            pe.wait_ge(s_ones, 2)

            def transposes(section, b, step, ch, src):
                bank_free(pe, section, b, step, ch)
                for u in range(PER):
                    last = nc.tensor.transpose(bank(section, step, ch)[:, BLK * u:BLK * u + BLK], src(PER * ch + u), pk("ident"))
                last.then_inc(written(section, step, ch), 1)

            def prep(b):
                pe.wait_ge(s_chst, b + 1)
                bank_free(pe, "prep", b, "gn", 0)
                mm(bank("prep", "gn", 0)[:, 0:1], pk("gmat"), MV[:, 0, 0:1], start=True, stop=True).then_inc(written("prep", "gn", 0), 1)
                pe.wait_ge(s_chsq, b + 1)
                bank_free(pe, "prep", b, "gn", 1)
                mm(bank("prep", "gn", 1)[:, 0:1], pk("gmat"), SM[:, 2:3], start=True, stop=True).then_inc(written("prep", "gn", 1), 1)
                pe.wait_ge(s_xn, b + 1)
                for ch in range(NCH):
                    i = 2 * ch
                    bank_free(pe, "prep", b, "e", i)
                    mm(bank("prep", "e", i), pk("w12"), XN[:, CHUNK * ch:CHUNK * ch + CHUNK], start=True, stop=True)\
                        .then_inc(written("prep", "e", i), 1)
                    bank_free(pe, "prep", b, "e", i + 1)
                    for u in range(PER):
                        t = CHUNK * ch + BLK * u
                        last = mm(bank("prep", "e", i + 1)[:, BLK * u:BLK * u + BLK], XN[:, t:t + BLK], pk("wa"), start=True, stop=True)
                    last.then_inc(written("prep", "e", i + 1), 1)
                wait_alone(pe, s_em, b + 1)
                with pe.Fori(0, 4) as h:
                    for ib in range(NBLK):
                        wait_alone(pe, s_mxd, b * (4 * NBLK) + h * NBLK + ib + 1)
                        for u in range(2):
                            for e2 in (E2H, E2M):
                                last = mm(PS[:, 2 * (ib % 4) + u, :], E1P[:, BLK * ib:BLK * ib + BLK],
                                          e2[:, bass.ds(h * 1024 + 512 * u, 512)], start=(e2 is E2H), stop=(e2 is E2M))
                        last.then_inc(s_mxq, 1)
                pe.wait_ge(s_m1, b + 1)
                bank_free(pe, "prep", b, "max")
                nc.tensor.transpose(bank("prep", "max")[0:NBLK, 0:128], M1[:, :], pk("ident")).then_inc(written("prep", "max"), 1)

            def scores(b, p, slot, banks):
                pe.wait_ge(s_cr, b * PAIRS + p + 1)
                if banks == 2 and not (isinstance(b, int) and b == 0):
                    wait_alone(pe, s_pe, b * PAIRS + p + 1)
                elif not (isinstance(p, int) and p < 1):
                    wait_alone(pe, s_pe, p)
                qc = cols(p)[0]
                for u in range(PAIR):
                    last = mm(PS[:, banks + u, :], E2R[:, slot, BLK * u:BLK * u + BLK], E1[:, bass.ds(qc, CHUNK)],
                              start=True, stop=True)
                last.then_inc(s_qk, 1)

            def values(b, p, slot):
                pe.wait_ge(s_pe, b * PAIRS + p + 2)
                pe.wait_ge(s_ca, b * PAIRS + p + 1)
                for u in range(PAIR):
                    last = mm(PVB, VR[:, slot, BLK * u:BLK * u + BLK], PROB[:, slot % 2, u, :],
                              start=(u == 0), stop=(u == PAIR - 1))
                last.then_inc(s_pv, 1)

            def conv_alone():
                pe.wait_ge(s_nmr, 16)

                def pair(p, slot, first):
                    scores(0, p, slot, 2 - 2 * (slot % 2))
                    if not first:
                        values(0, p - 1, (slot - 1) % PER)

                alone_pairs(pe, pair)
                values(0, PAIRS - 1, 3)

            def finalize(b):
                pe.wait_ge(s_ps, b * PAIRS + PAIRS + 2)
                pe.wait_ge(s_ca, b * PAIRS + PAIRS + 1)
                bank_free(pe, "fin", b, "den")
                for i in range(NBLK):
                    last = mm(bank("fin", "den")[:, i:i + 1], SA[:, BLK * i:BLK * i + BLK], ONES[:, 0:1], start=True, stop=True)
                last.then_inc(written("fin", "den"), 1)
                bank_read(pe, "fin", b, "den")
                bank_free(pe, "fin", b, "row")
                nc.tensor.transpose(bank("fin", "row")[0:NBLK, 0:128], M1[:, :], pk("ident")).then_inc(written("fin", "row"), 1)
                pe.wait_ge(s_rrl, 16 * b + 16)
                for ch in range(NCH):
                    bank_free(pe, "fin", b, "bc", ch)
                    mm(bank("fin", "bc", ch), ONES[HALF:HALF + 1, :], E1[HALF:HALF + 1, CHUNK * ch:CHUNK * ch + CHUNK],
                       start=True, stop=True).then_inc(written("fin", "bc", ch), 1)

            def norm(b):
                for ch in range(NCH):
                    pe.wait_ge(s_cx, NCH * b + ch + 1)
                    transposes("ln", b, "t", ch, lambda i: X[:, BLK * i:BLK * i + BLK])
                for ch in range(NCH):
                    pe.wait_ge(s_xt, 2 * b * NBLK + PER * (ch + 1))
                    transposes("ln", b, "c", ch, lambda i: XT[:, i, :])
                for ch in range(NCH):
                    bank_free(pe, "ln", b, "f", ch)
                    mm(bank("ln", "f", ch), pk("w1a"), XN[:, CHUNK * ch:CHUNK * ch + CHUNK], start=True, stop=True)\
                        .then_inc(written("ln", "f", ch), 1)
                bank_free(pe, "ln", b, "b")
                for r in range(KEYS):
                    last = mm(bank("ln", "b"), w1b[:, r, :], XN[:, r:TOK:KEYS], start=(r == 0), stop=(r == KEYS - 1))
                last.then_inc(written("ln", "b"), 1)

            def attend(b, conv):
                def finish(prev):
                    m = b * NB + prev.n
                    w = CHUNK - prev.off
                    if prev.diag is None:
                        pe.wait_ge(s_ex, m + 1)
                    else:
                        pe.wait_ge(s_mk, b * NBLK + PER * prev.c + prev.diag + 1)
                    pe.wait_ge(s_vr, m + 1)
                    if prev.first:
                        pe.wait_ge(s_da, b * NCH + prev.c + 1)
                    mm(ACC[:, prev.off:CHUNK], XR[:, prev.ring, :], EB[:, prev.par, 0:w],
                       start=prev.first, stop=True, skip_group_check=True).then_inc(s_ep, 1)
                    if prev.last:
                        pe.wait_ge(s_es, m + 3)
                        pe.wait_ge(s_dd, b * NCH + prev.c + 1)
                        mm(DEN, ONES[:, :], DS[:, prev.c % 2, :], start=True, stop=True).then_inc(s_dc, 1)

                def step(cur, prev):
                    if cur is None:
                        finish(prev)
                        return
                    p = beside(cur) if conv else None
                    p1 = beside(prev) if conv and prev is not None else None
                    if p1 is not None:
                        values(b + 1, p1, prev.ring)
                    n = b * NB + cur.n
                    w = CHUNK - cur.off
                    for k in range(UNITS):
                        pe.wait_ge(s_th, UNITS * n + k + 1)
                        for q in range(4):
                            last = mm(PS[32 * q:32 * q + 32, cur.par, 0:w], w2k[:, k, :], S[:, k, q, 0:w],
                                      start=(k == 0), stop=(k == UNITS - 1))
                        last.then_inc(s_tu, 1)
                        if k == 1 and p is not None:
                            scores(b + 1, p, cur.ring, 2)
                        if k == 2 and prev is not None:
                            finish(prev)

                if conv:
                    pe.wait_ge(s_nmr, 16 * b + 32)
                each_block(pe, step)

            def gate(b):
                pe.wait_ge(s_dx, NCH * (b + 1))
                for ch in range(NCH):
                    transposes("gate", b, "t", ch, lambda i: X[:, BLK * i:BLK * i + BLK])
                for ch in range(NCH):
                    pe.wait_ge(s_xt, (2 * b + 1) * NBLK + PER * (ch + 1))
                    transposes("gate", b, "c", ch, lambda i: XT[:, i, :])
                for ch in range(NCH):
                    bank_free(pe, "gate", b, "l", ch)
                    mm(bank("gate", "l", ch)[0:EXP, :], pk("gw"), XC2[:, CHUNK * ch:CHUNK * ch + CHUNK], start=True, stop=True)\
                        .then_inc(written("gate", "l", ch), 1)
                pe.wait_ge(s_sp, b + 1)
                for t in range(4):
                    bank_free(pe, "gate", b, "p", t, alone=True)
                    for u in range(8):
                        i = 8 * t + u
                        last = nc.tensor.transpose(bank("gate", "p", t)[:, EXP * u:EXP * u + EXP], SELP[:, BLK * i:BLK * i + BLK],
                                                   pk("ident", EXP)[:, 0:EXP])
                    last.then_inc(written("gate", "p", t), 1)
                pe.wait_ge(s_pt, 4 * (b + 1))
                bank_free(pe, "gate", b, "pl")
                for i in range(NBLK):
                    last = mm(bank("gate", "pl")[:, 0:EXP], XT[:, i, :], PT[:, i, :], start=(i == 0), stop=(i == NBLK - 1))
                last.then_inc(written("gate", "pl"), 1)

            schedule(pe, prep, conv_alone, finalize, norm, attend, gate)

            pe.wait_ge(s_pl, BATCH)
            pe.wait_ge(s_ec, 48)

            def up(g):
                pe.wait_ge(s_w[g % len(WG)], 16 * (g // len(WG) + 1))
                if g >= 2:
                    pe.wait_ge(s_g, g - 1)
                mm(PS[:, g % 2, :], SELB[:, 128 * g:128 * g + 128], B1A, start=True, stop=True, skip_group_check=True)
                for q in range(4):
                    last = mm(PS[32 * q:32 * q + BATCH, g % 2, :], PL[:, 4 * g + q, :], W1G[g % len(WG)][:, q, :],
                              start=False, stop=True, skip_group_check=True)
                last.then_inc(s_h, 1)

            def down(g):
                pe.wait_ge(s_g, g + 1)
                if g >= 1:
                    pe.wait_ge(s_htc, g)
                for c in range(4):
                    last = nc.tensor.transpose(PS[:, 2, BLK * c:BLK * c + BLK], HS[:, BLK * c:BLK * c + BLK], pk("ident"))
                last.then_inc(s_ht, 1)
                pe.wait_ge(s_htc, g + 1)
                if g >= 2:
                    pe.wait_ge(s_oc, g - 1)
                mm(PS[:, 4 + g % 2, 0:OUT], SELB[:, 128 * g:128 * g + 128], B2A, start=True, stop=True, skip_group_check=True)
                for c in range(4):
                    for q in range(4):
                        last = mm(PS[32 * q:32 * q + BATCH, 4 + g % 2, 0:OUT], HT[:, c, 32 * q:32 * q + BATCH],
                                  W2G[g % len(WG)][:, q, c, :], start=False, stop=True, skip_group_check=True)
                last.then_inc(s_wu, 1)

            up(0)
            for g in range(GRP):
                if g + 1 < GRP:
                    up(g + 1)
                down(g)
            pe.wait_ge(s_eol, 16)
            pe.wait_ge(s_oc, GRP)
            for b in range(BATCH):
                pe.wait_ge(s_fl[b % 2], 32 * (b // 2 + 1))
                for ch in range(NCH):
                    i = NCH * b + ch
                    if i >= 8:
                        pe.wait_ge(s_fa, i - 7)
                    mm(PS[:, i % 8, :], EO[:, b, :], PF[b % 2][:, CHUNK * ch:CHUNK * ch + CHUNK], start=True, stop=True)\
                        .then_inc(s_fm, 1)

        @block.vector
        def _(dve):
            v = nc.vector
            STEPS = {"prep": 35, "fin": 1, "norm": 17, "attend": 24, "gate": 22}
            at = {}

            def steps_before(section, b):
                pro = STEPS["prep"] + STEPS["fin"]
                it = sum(STEPS.values())
                upto = {"norm": [], "prep": ["norm"], "attend": ["norm", "prep"], "gate": ["norm", "prep", "attend"],
                        "fin": ["norm", "prep", "attend", "gate"]}[section]
                if section in ("prep", "fin"):
                    if isinstance(b, int) and b == 0:
                        return 0 if section == "prep" else STEPS["prep"]
                    b = b - 1
                elif isinstance(b, int) and b == BATCH - 1:
                    upto = [k for k in upto if k != "prep"]
                return b * it + (pro + sum(STEPS[k] for k in upto))

            def linker(section, b):
                start = steps_before(section, b)
                at[section] = 0

                def link(ins, alone=False):
                    at[section] += 1
                    ins.then_inc(s_v, 1)
                    (wait_alone if alone else wait)(dve, s_v, start + at[section])

                return link

            def prep(b):
                link = linker("prep", b)
                dve.wait_ge(s_x, 16 * b + 16)
                for ch in range(NCH):
                    last = v.bn_stats(ST[:, ch, :], XN[:, CHUNK * ch:CHUNK * ch + CHUNK])
                link(last, alone=True)
                v.bn_aggr(MV[:, 0, :], ST[:, 0:NCH, :]).then_inc(s_chst, 1)
                bank_ready(dve, "prep", b, "gn", 0)
                v.tensor_copy(SM[:, 0:1], bank("prep", "gn", 0)[:, 0:1]).then_inc(used("prep", "gn", 0), 1)
                bank_read(dve, "prep", b, "gn", 0)
                link(v.tensor_tensor(SM[:, 1:2], MV[:, 0, 0:1], SM[:, 0:1], ALU.subtract))
                v.scalar_tensor_tensor(SM[:, 2:3], SM[:, 1:2], SM[:, 1:2], MV[:, 0, 1:2], ALU.mult, ALU.add).then_inc(s_chsq, 1)
                bank_ready(dve, "prep", b, "gn", 1)
                v.tensor_copy(SM[:, 7:8], bank("prep", "gn", 1)[:, 0:1]).then_inc(used("prep", "gn", 1), 1)
                bank_read(dve, "prep", b, "gn", 1)
                v.tensor_scalar(SM[:, 3:4], SM[:, 7:8], GN_EPS, None, ALU.add).then_inc(s_gv, 1)
                dve.wait_ge(s_gd, b + 1)
                link(v.reciprocal(SM[:, 5:6], SM[:, 4:5]))
                v.tensor_scalar(XN[:, :], XN[:, :], SM[:, 0:1], SM[:, 5:6], ALU.subtract, ALU.mult).then_inc(s_xn, 1)
                for ch in range(NCH):
                    i, t = 2 * ch, slice(CHUNK * ch, CHUNK * ch + CHUNK)
                    bank_ready(dve, "prep", b, "e", i)
                    y = bank("prep", "e", i)
                    link(v.tensor_scalar(T1[:, :], y, pk("b12"), 0.0, ALU.add, ALU.min))
                    v.tensor_scalar(T2[:, :], y, pk("b12"), 0.0, ALU.add, ALU.max).then_inc(used("prep", "e", i), 1)
                    bank_read(dve, "prep", b, "e", i)
                    v.scalar_tensor_tensor(E1[0:HALF, t], T1[0:HALF, :], pk("a12")[0:HALF], T2[0:HALF, :], ALU.mult, ALU.add)
                    link(v.scalar_tensor_tensor(E2[:, t], T1[HALF:, :], pk("a12")[HALF:], T2[HALF:, :], ALU.mult, ALU.add))
                    bank_ready(dve, "prep", b, "e", i + 1)
                    y = bank("prep", "e", i + 1).rearrange("p (u c) -> p u c", u=PER)
                    t1, t2 = (z[:, :].rearrange("p (u c) -> p u c", u=PER) for z in (T1, T2))
                    v.tensor_tensor(t2, y, pk("ba")[:, None, :].to_broadcast([128, PER, 128]), ALU.add)\
                        .then_inc(used("prep", "e", i + 1), 1)
                    bank_read(dve, "prep", b, "e", i + 1)
                    link(v.tensor_scalar(t1, t2, 0.0, pk("aa"), ALU.min, ALU.mult))
                    last = v.scalar_tensor_tensor(VT[:, PER * ch:PER * ch + PER, :], t2, 0.0, t1, ALU.max, ALU.add)
                    if ch < NCH - 1:
                        link(last)
                last.then_inc(s_ea, 1)
                dve.wait_ge(s_eh, 3 * b + 1)
                v.tensor_tensor(E1P[HALF:, :], E1[0:HALF, :], E1P[0:HALF, :], ALU.subtract)
                dve.wait_ge(s_eh, 3 * b + 2)
                v.tensor_tensor(E2M[0:HALF, :], E2[:, :], E2H[0:HALF, :], ALU.subtract)
                dve.wait_ge(s_eh, 3 * b + 3)
                v.tensor_tensor(E2M[HALF:, :], E2[:, :], E2H[0:HALF, :], ALU.subtract).then_inc(s_em, 1)
                with dve.Fori(0, 4) as h:
                    for ib in range(NBLK):
                        dve.wait_ge(s_mxq, b * (4 * NBLK) + h * NBLK + (ib + 1))
                        v.tensor_reduce(MX[:, ib, bass.ds(h, 1)], PS[:, 2 * (ib % 4):2 * (ib % 4) + 2, :]
                                        .rearrange("p u n -> p (u n)"), AXX, ALU.max).then_inc(s_mxd, 1)
                dve.wait_ge(s_mxd, b * (4 * NBLK) + 4 * NBLK + 4)
                v.tensor_reduce(M1[:, :], MX[:, :, :], AXX, ALU.max).then_inc(s_m1, 1)
                bank_ready(dve, "prep", b, "max")
                link(v.tensor_scalar(NM[:, :], bank("prep", "max")[0:NBLK, 0:128], -1.0, None, ALU.mult))
                dve.sem_inc(s_nm, 1)
                dve.sem_inc(used("prep", "max"), 1)
                assert at["prep"] == STEPS["prep"], at

            def rings(b, p, slot):
                wait_alone(dve, s_pv, b * PAIRS + p + 1)
                kc = cols(p)[1]
                v.tensor_copy(E2R[0:HALF, slot, :], E2[:, bass.ds(kc, PAIR * BLK)])
                v.tensor_copy(VR[:, slot, :], XC2[:, bass.ds(kc, PAIR * BLK)]).then_inc(s_cr, 1)

            def conv_add(b, p):
                dve.wait_ge(s_pv, b * PAIRS + p + 5)
                dve.wait_ge(s_ca, b * PAIRS + p + 1)
                cc = CA[:, bass.ds(cols(p)[0], CHUNK)]
                v.tensor_tensor(cc, cc, PVB, ALU.add).then_inc(s_ca, 1)

            def conv_alone():
                dve.wait_ge(s_cz, 2)

                def pair(p, slot, first):
                    rings(0, p, slot)
                    if not (isinstance(p, int) and p < 2):
                        conv_add(0, p - 2)

                alone_pairs(dve, pair)
                conv_add(0, PAIRS - 2)
                conv_add(0, PAIRS - 1)

            def finalize(b):
                link = linker("fin", b)
                bank_ready(dve, "fin", b, "den")
                v.reciprocal(M1[:, :], bank("fin", "den")[:, 0:NBLK]).then_inc(used("fin", "den"), 1)
                bank_ready(dve, "fin", b, "row")
                link(v.tensor_copy(NM[:, :], bank("fin", "row")[0:NBLK, 0:128]))
                dve.sem_inc(s_rr, 1)
                dve.sem_inc(used("fin", "row"), 1)
                dve.wait_ge(s_xr, 16 * b + 16)
                for ch in range(NCH):
                    t = slice(CHUNK * ch, CHUNK * ch + CHUNK)
                    bank_ready(dve, "fin", b, "bc", ch)
                    v.tensor_tensor(CA[:, t], CA[:, t], bank("fin", "bc", ch), ALU.mult).then_inc(used("fin", "bc", ch), 1)
                    bank_read(dve, "fin", b, "bc", ch)
                    v.tensor_tensor(X[:, t], X[:, t], CA[:, t], ALU.add).then_inc(s_cx, 1)
                assert at["fin"] == STEPS["fin"], at

            def layer_norm(section, b, j, link):
                for ch in range(NCH):
                    bank_ready(dve, section, b, "t", ch)
                    y = bank(section, "t", ch)
                    for u in range(PER):
                        last = v.bn_stats(ST[:, PER * ch + u, :], y[:, BLK * u:BLK * u + BLK])
                    link(last)
                    v.tensor_copy(XT[:, PER * ch:PER * ch + PER, :],
                                  y.rearrange("p (u c) -> p u c", u=PER)).then_inc(used(section, "t", ch), 1)
                    for u in range(PER):
                        last = v.bn_aggr(MV[:, PER * ch + u, :], ST[:, PER * ch + u, :])
                    link(last)
                bank_read(dve, section, b, "t", NCH - 2)
                bank_read(dve, section, b, "t", NCH - 1)
                v.tensor_scalar(RS[:, :], MV[:, :, 1], LN_EPS, None, ALU.add).then_inc(s_lv, 1)
                dve.wait_ge(s_ld, 2 * b + 1 + j)
                link(v.reciprocal(RS[:, :], RS[:, :]))
                for i in range(NBLK):
                    v.tensor_scalar(XT[:, i, :], XT[:, i, :], MV[:, i, 0:1], RS[:, i:i + 1], ALU.subtract, ALU.mult)\
                        .then_inc(s_xt, 1)

            def norm(b):
                link = linker("norm", b)
                dve.wait_ge(s_cx, (b + 1) * NCH)
                layer_norm("ln", b, 0, link)
                bank_read(dve, "ln", b, "f", NCH - 2)
                bank_read(dve, "ln", b, "f", NCH - 1)
                bank_read(dve, "ln", b, "b")
                dve.sem_inc(s_kr, 1)
                assert at["norm"] == STEPS["norm"], at

            def attend(b, conv):
                link = linker("attend", b)

                def take_chunk(c):
                    dve.wait_ge(s_dc, b * NCH + c + 1)
                    v.tensor_copy(ACCS[:, :], ACC).then_inc(s_da, 1)
                    v.tensor_scalar(RD[:, :], DEN, DEN_EPS, None, ALU.add).then_inc(s_dd, 1)

                def invert(c, half):
                    dve.wait_ge(s_dd, b * NCH + c + 2)
                    h = slice(half * CHUNK // 2, (half + 1) * CHUNK // 2)
                    link(v.reciprocal(RD[:, h], RD[:, h]))

                def add_context(c):
                    dve.wait_ge(s_da, b * NCH + c + 2)
                    link(v.tensor_tensor(T1[:, :], ACCS[:, :], RD[:, :], ALU.mult))
                    xc = X[:, CHUNK * c:CHUNK * c + CHUNK]
                    v.tensor_tensor(xc, xc, T1[:, :], ALU.add).then_inc(s_dx, 1)

                def step(cur, prev):
                    before_this = None
                    if cur is not None and cur.c > 0 and isinstance(cur.jb, int) and cur.jb < PER:
                        before_this = cur.c - 1
                    if cur is not None:
                        n = b * NB + cur.n
                        w = CHUNK - cur.off
                        q0 = CHUNK * cur.c + cur.off
                        if conv and beside(cur) is not None:
                            rings(b + 1, beside(cur), cur.ring)
                        if cur.ring == 0:
                            dve.wait_ge(s_sum, UNITS * n + 1)
                            v.tensor_copy(BR[:, :, :].rearrange("p u k -> p (u k)"),
                                          B[:, bass.ds(cur.jb * 16, PER * 16)]).then_inc(s_br, 1)
                            dve.wait_ge(s_br, (b * NB + cur.n) // PER + 1)
                        for k in range(UNITS):
                            dve.wait_ge(s_tu, UNITS * n + k + 1)
                            if before_this is not None and cur.jb == 1 and k == 3:
                                take_chunk(before_this)
                            for q in range(4):
                                last = v.tensor_scalar(S[:, k, q, 0:w], F[:, q0:q0 + w],
                                                       BR[:, cur.ring, 4 * q + k:4 * q + k + 1], None, ALU.add)
                            last.then_inc(s_sum, 1)
                    if prev is not None and prev.diag is not None:
                        dve.wait_ge(s_ex, b * NB + prev.n + 1)
                        e = EB[:, prev.par, 0:BLK]
                        v.tensor_tensor(e, e, pk("tri"), ALU.mult).then_inc(s_mk, 1)
                    p = beside(prev) if conv and prev is not None else None
                    if p is not None:
                        conv_add(b + 1, p)
                    if before_this is not None and cur.jb in (1, 2):
                        invert(before_this, cur.jb - 1)
                    if before_this is not None and cur.jb == 3:
                        add_context(before_this)
                    if cur is None:
                        take_chunk(prev.c)
                        invert(prev.c, 0)
                        invert(prev.c, 1)
                        add_context(prev.c)

                if conv:
                    dve.wait_ge(s_cz, 2 * b + 4)
                each_block(dve, step)
                dve.wait_ge(s_dx, (b + 1) * NCH)
                assert at["attend"] == STEPS["attend"], at

            def gate(b):
                link = linker("gate", b)
                layer_norm("gate", b, 1, link)
                for ch in range(NCH):
                    bank_ready(dve, "gate", b, "l", ch)
                    v.tensor_scalar(LOG[:, CHUNK * ch:CHUNK * ch + CHUNK], bank("gate", "l", ch)[0:EXP, :],
                                    pk("gb", EXP), None, ALU.add).then_inc(used("gate", "l", ch), 1)
                bank_read(dve, "gate", b, "l", NCH - 2)
                bank_read(dve, "gate", b, "l", NCH - 1)
                link(v.tensor_reduce(SM[0:EXP, 4:5], LOG, AXX, ALU.max))
                v.tensor_scalar(SM[0:EXP, 5:6], SM[0:EXP, 4:5], -1.0, None, ALU.mult).then_inc(s_lx, 1)
                dve.wait_ge(s_le, b + 1)
                link(v.reciprocal(SM[0:EXP, 7:8], SM[0:EXP, 6:7]))
                link(v.tensor_scalar(LOG, LOG, SM[0:EXP, 7:8], None, ALU.mult), alone=True)
                link(v.max(TOP, LOG), alone=True)
                link(v.match_replace(REM, TOP, LOG, 0.0))
                v.tensor_tensor(SELP, LOG, REM, ALU.subtract).then_inc(s_sp, 1)
                for t in range(4):
                    bank_ready(dve, "gate", b, "p", t)
                    v.tensor_copy(PT[:, 8 * t:8 * t + 8, :], bank("gate", "p", t).rearrange("p (k e) -> p k e", e=EXP))\
                        .then_inc(used("gate", "p", t), 1)
                bank_read(dve, "gate", b, "p", 2)
                bank_read(dve, "gate", b, "p", 3)
                dve.sem_inc(s_pt, 4)
                bank_ready(dve, "gate", b, "pl")
                v.tensor_copy(PL[:, :, bass.ds(b, 1)], bank("gate", "pl")[:, 0:EXP][:, :, None]).then_inc(used("gate", "pl"), 1)
                bank_read(dve, "gate", b, "pl")
                dve.sem_inc(s_pl, 1)
                assert at["gate"] == STEPS["gate"], at

            dve.wait_ge(s_const, 16)
            schedule(dve, prep, conv_alone, finalize, norm, attend, gate)
            for g in range(GRP):
                dve.wait_ge(s_ht, g + 1)
                if g >= 1:
                    dve.wait_ge(s_wu, g)
                v.tensor_copy(HT, PS[:, 2, :].rearrange("p (c m) -> p c m", c=4)).then_inc(s_htc, 1)
                dve.wait_ge(s_wu, g + 1)
                v.tensor_copy(ES[:, g, :], PS[:, 4 + g % 2, 0:OUT]).then_inc(s_oc, 1)
            for b in range(BATCH):
                for ch in range(NCH):
                    i = NCH * b + ch
                    dve.wait_ge(s_fm, i + 1)
                    yc = YF[b % 2][:, CHUNK * ch:CHUNK * ch + CHUNK]
                    v.tensor_tensor(yc, yc, PS[:, i % 8, :], ALU.add).then_inc(s_fa, 1)


def kernel(**inputs):
    import numpy as np
    import concourse.bacc as _bacc
    from concourse import mybir as _mybir
    from concourse.bass_utils import run_bass_kernel_spmd as _run

    a = {k: np.ascontiguousarray(v) for k, v in inputs.items()}
    pack = np.zeros((128, NPACK), np.float32)

    def put(name, value, rows=128):
        s, e = _AT[name]
        pack[0:rows, s:e] = value

    put("ident", np.eye(128, dtype=np.float32))
    put("gmat", np.kron(np.eye(32, dtype=np.float32), np.full((4, 4), 0.25, np.float32)))
    put("tri", np.triu(np.ones((128, 128), np.float32), 1))
    put("w12", np.concatenate([a["L0_conv_w1"].T, a["L0_conv_w2"].T], axis=1))
    put("wa", a["L0_conv_wa"].T)
    put("gw", a["L1_ffn_gate_w"].T)
    W1 = a["L1_attn_W1"]
    put("w1a", np.tile(W1[0:128], (1, 8)))
    w1b = np.zeros((128, 8, 8, 16), np.float32)
    w2k = np.zeros((8, 16, 4, 4, 8), np.float32)
    for r in range(8):
        w1b[:, r, r, :] = W1[128:256]
        for k in range(4):
            w2k[r, :, k, k, r] = a["L1_attn_w2"][:, 0]
    put("w1b", w1b.reshape(128, -1))
    put("w2k", w2k.reshape(128, -1))
    put("ba", np.broadcast_to(a["L0_conv_ba"], (128, 128)))
    put("b12", np.concatenate([a["L0_conv_b1"], a["L0_conv_b2"]])[:, None])
    put("a12", np.concatenate([np.broadcast_to(a["L0_conv_a1"], (64,)), np.broadcast_to(a["L0_conv_a2"], (64,))])[:, None])
    put("b1", np.tile(a["L1_attn_b1"], 8)[:, None])
    put("b2", np.broadcast_to(a["L1_attn_b2"], (128, 1)))
    put("aa", np.broadcast_to(a["L0_conv_aa"], (128, 1)))
    put("gb", a["L1_ffn_gate_b"][:, None], 64)
    arrays = {
        "x": a["x"].reshape(BATCH, CH, TOK),
        "pack": pack,
        "sel": np.repeat(np.eye(EXP, dtype=np.float32), 32, axis=1),
        "wg": np.ascontiguousarray(np.concatenate([
            a["L1_ffn_weight1"][:, 0:CH, :].reshape(GRP, 4, CH, HID).transpose(0, 2, 1, 3).reshape(GRP, 128, -1),
            a["L1_ffn_weight2"][:, 0:HID, :].reshape(GRP, 4, 4, 128, OUT).transpose(0, 3, 1, 2, 4).reshape(GRP, 128, -1),
        ], axis=2)),
        "b1all": np.ascontiguousarray(a["L1_ffn_weight1"][:, CH, :]),
        "b2all": np.ascontiguousarray(a["L1_ffn_weight2"][:, HID, :]),
    }
    nc = _bacc.Bacc("TRN2", target_bir_lowering=False, num_devices=1)
    f32 = _mybir.dt.float32
    args = [nc.dram_tensor(f"in_{k}", v.shape, f32, kind="ExternalInput").ap() for k, v in arrays.items()]
    args.append(nc.dram_tensor("out_0", (BATCH, CH, TOK), f32, kind="ExternalOutput").ap())
    args.append(nc.dram_tensor("y2_scratch", (BATCH, CH, TOK), f32, kind="Internal").ap())
    args.append(nc.dram_tensor("p_scratch", (BATCH, EXP, TOK), f32, kind="Internal").ap())
    args.append(nc.dram_tensor("eo_scratch", (BATCH, EXP, OUT), f32, kind="Internal").ap())
    hybrid_kernel(nc, *args)
    r = _run(nc, [{f"in_{k}": v for k, v in arrays.items()}], core_ids=[0])
    return r.results[0]["out_0"].reshape(BATCH, CH, 64, 64)
```
